# Optimizing a Trainium2 kernel written in Bass

```python
import numpy as np
import jax
import jax.numpy as jnp

def _softmax(x, axis=-1):
    return jax.nn.softmax(x, axis=axis)

def _gelu(x):
    return jax.nn.gelu(x, approximate=True)

def _silu(x):
    return jax.nn.silu(x)

def _sigmoid(x):
    return jax.nn.sigmoid(x)

def _layernorm(x, axis=-1, eps=1e-05):
    m = jnp.mean(x, axis=axis, keepdims=True)
    v = jnp.var(x, axis=axis, keepdims=True)
    return (x - m) / jnp.sqrt(v + eps)

def _scatter_add(tgt, idx, src, axis=0):
    return tgt.at[idx].add(src)

def _segment_sum(src, seg, n):
    return jax.ops.segment_sum(src, seg, n)
kernel_name = 'mk_flamingo_gated_d1_seqx_r8_511eba'

def setup_inputs(seed: int=0):
    np.random.seed(seed)
    _w = jnp.asarray

    def _rec_inputs():
        import jax
        import jax.numpy as jnp
        _rk = jax.random.key(seed)
        x = 0.0001212 + 1 * jax.random.normal(jax.random.fold_in(_rk, 1), (8, 128, 512), jnp.float32)
        _lenS = 128 - jax.random.randint(jax.random.fold_in(_rk, 7), (8,), 0, max(1, 128 // 4) + 1, jnp.int32)
        _lenS2 = 128 - jax.random.randint(jax.random.fold_in(_rk, 8), (8,), 0, max(1, 128 // 4) + 1, jnp.int32)
        _ctx_4096P = jax.random.normal(jax.random.fold_in(_rk, 11), (8, 16, 512), jnp.float32)
        _ctx_4096c = jax.random.dirichlet(jax.random.fold_in(_rk, 511), 0.3 * jnp.ones((16,), jnp.float32), (8, 128))
        _ctx_4096t = jnp.einsum('bsk,bkd->bsd', _ctx_4096c, _ctx_4096P)
        _ctx_4096t = _ctx_4096t * jax.lax.rsqrt(jnp.mean(jnp.square(_ctx_4096t)) + 1e-12) * 0.953939
        ctx_4096 = -0.000125008 + 0.999885 * (_ctx_4096t + 0.3 * jax.random.normal(jax.random.fold_in(_rk, 611), (8, 128, 512), jnp.float32))
        _g = jax.random.normal(jax.random.fold_in(_rk, 9001), (2, 1), jnp.float32)
        _g = jnp.sign(_g) * jnp.maximum(jnp.abs(_g), 1.0) + (_g == 0) * 1.0
        g_xattn = _g[0]
        g_ffn = _g[1]
        return (x, ctx_4096, g_xattn, g_ffn)
    x, ctx_4096, g_xattn, g_ffn = _rec_inputs()

    def _L0_xattn_setup():
        import jax, jax.numpy as jnp
        import numpy as np
        N, C, S = (16, 64, 512)
        rng = jax.random.key(seed)
        k1, k2, k3 = jax.random.split(rng, 3)
        return {'key': jax.random.normal(k1, (N, C, S), dtype=jnp.float32), 'value': jax.random.normal(k2, (N, C, S), dtype=jnp.float32), 'query': jax.random.normal(k3, (N, C, S), dtype=jnp.float32)}
    _L0_xattn_all = _L0_xattn_setup()
    _L0_xattn_in = {k: v for k, v in _L0_xattn_all.items() if k in ()}
    del _L0_xattn_all

    def _L0_ffn_setup():
        import jax, jax.numpy as jnp
        import numpy as np
        HID = 512
        INTER = 1376
        BITS = 4
        PACK = 8
        MAXQ = 15
        GROUP = 128

        def _dequant(qweight, scales, qzeros, g_idx):
            shifts = jnp.arange(PACK, dtype=jnp.uint32) * BITS
            qw = qweight.astype(jnp.uint32)
            w = (qw[:, None, :] >> shifts[None, :, None] & MAXQ).reshape(-1, qweight.shape[1])
            qz = qzeros.astype(jnp.uint32)
            z = ((qz[:, :, None] >> shifts[None, None, :] & MAXQ) + 1).reshape(qzeros.shape[0], -1)
            s = scales[g_idx]
            return (w.astype(scales.dtype) - z[g_idx].astype(scales.dtype)) * s
        key = jax.random.key(seed)
        ks = jax.random.split(key, 16)

        def qw(k, K, N):
            return jax.random.randint(k, (K // PACK, N), 0, 2147483647, dtype=jnp.int32)

        def qz(k, G, N):
            return jax.random.randint(k, (G, N // PACK), 0, 2147483647, dtype=jnp.int32)

        def sc(k, G, N):
            return jax.random.uniform(k, (G, N), jnp.float32, 0.001, 0.01)
        Gk = HID // GROUP
        Gd = INTER // GROUP
        return {'x': jax.random.normal(ks[0], (4, 256, HID), jnp.float32), 'gate_qweight': qw(ks[1], HID, INTER), 'gate_scales': sc(ks[2], Gk, INTER), 'gate_qzeros': qz(ks[3], Gk, INTER), 'gate_g_idx': (jnp.arange(HID) // GROUP).astype(jnp.int32), 'up_qweight': qw(ks[4], HID, INTER), 'up_scales': sc(ks[5], Gk, INTER), 'up_qzeros': qz(ks[6], Gk, INTER), 'up_g_idx': (jnp.arange(HID) // GROUP).astype(jnp.int32), 'down_qweight': qw(ks[7], INTER, HID), 'down_scales': sc(ks[8], Gd, HID), 'down_qzeros': qz(ks[9], Gd, HID), 'down_g_idx': (jnp.arange(INTER) // GROUP).astype(jnp.int32)}
    _L0_ffn_all = _L0_ffn_setup()
    _L0_ffn_in = {k: v for k, v in _L0_ffn_all.items() if k in ('gate_qweight', 'gate_scales', 'gate_qzeros', 'gate_g_idx', 'up_qweight', 'up_scales', 'up_qzeros', 'up_g_idx', 'down_qweight', 'down_scales', 'down_qzeros', 'down_g_idx')}
    del _L0_ffn_all
    return {'x': x, 'ctx_4096': ctx_4096, 'g_xattn': g_xattn, 'g_ffn': g_ffn, 'L0_ffn_gate_qweight': _L0_ffn_in['gate_qweight'], 'L0_ffn_gate_scales': _L0_ffn_in['gate_scales'], 'L0_ffn_gate_qzeros': _L0_ffn_in['gate_qzeros'], 'L0_ffn_gate_g_idx': _L0_ffn_in['gate_g_idx'], 'L0_ffn_up_qweight': _L0_ffn_in['up_qweight'], 'L0_ffn_up_scales': _L0_ffn_in['up_scales'], 'L0_ffn_up_qzeros': _L0_ffn_in['up_qzeros'], 'L0_ffn_up_g_idx': _L0_ffn_in['up_g_idx'], 'L0_ffn_down_qweight': _L0_ffn_in['down_qweight'], 'L0_ffn_down_scales': _L0_ffn_in['down_scales'], 'L0_ffn_down_qzeros': _L0_ffn_in['down_qzeros'], 'L0_ffn_down_g_idx': _L0_ffn_in['down_g_idx']}

def reference(x, ctx_4096, g_xattn, g_ffn, L0_ffn_gate_qweight, L0_ffn_gate_scales, L0_ffn_gate_qzeros, L0_ffn_gate_g_idx, L0_ffn_up_qweight, L0_ffn_up_scales, L0_ffn_up_qzeros, L0_ffn_up_g_idx, L0_ffn_down_qweight, L0_ffn_down_scales, L0_ffn_down_qzeros, L0_ffn_down_g_idx):
    import jax
    import jax.numpy as jnp

    def _L0_xattn_ref(key, value, query):
        import jax, jax.numpy as jnp
        import numpy as np
        N, C, S = (16, 64, 512)
        KC = key.shape[1]
        sim = jnp.einsum('ncs,nds->ncd', key, query) * KC ** (-0.5)
        sim = jax.nn.softmax(sim, axis=1)
        context = jnp.einsum('ncd,nds->ncs', sim, value)
        return context

    def _L0_ffn_ref(x, gate_qweight, gate_scales, gate_qzeros, gate_g_idx, up_qweight, up_scales, up_qzeros, up_g_idx, down_qweight, down_scales, down_qzeros, down_g_idx):
        import jax, jax.numpy as jnp
        import numpy as np
        HID = 512
        INTER = 1376
        BITS = 4
        PACK = 8
        MAXQ = 15
        GROUP = 128

        def _dequant(qweight, scales, qzeros, g_idx):
            shifts = jnp.arange(PACK, dtype=jnp.uint32) * BITS
            qw = qweight.astype(jnp.uint32)
            w = (qw[:, None, :] >> shifts[None, :, None] & MAXQ).reshape(-1, qweight.shape[1])
            qz = qzeros.astype(jnp.uint32)
            z = ((qz[:, :, None] >> shifts[None, None, :] & MAXQ) + 1).reshape(qzeros.shape[0], -1)
            s = scales[g_idx]
            return (w.astype(scales.dtype) - z[g_idx].astype(scales.dtype)) * s
        Wg = _dequant(gate_qweight, gate_scales, gate_qzeros, gate_g_idx)
        Wu = _dequant(up_qweight, up_scales, up_qzeros, up_g_idx)
        Wd = _dequant(down_qweight, down_scales, down_qzeros, down_g_idx)
        xf = x.reshape(-1, x.shape[-1])
        h = jax.nn.silu(xf @ Wg) * (xf @ Wu)
        out = h @ Wd
        return out.reshape(x.shape[:-1] + (Wd.shape[1],))
    x = x + jnp.tanh(g_xattn[0]) * _L0_xattn_ref(ctx_4096, ctx_4096, _layernorm(x, axis=-1))
    x = x + jnp.tanh(g_ffn[0]) * _L0_ffn_ref(_layernorm(x, axis=-1), L0_ffn_gate_qweight, L0_ffn_gate_scales, L0_ffn_gate_qzeros, L0_ffn_gate_g_idx, L0_ffn_up_qweight, L0_ffn_up_scales, L0_ffn_up_qzeros, L0_ffn_up_g_idx, L0_ffn_down_qweight, L0_ffn_down_scales, L0_ffn_down_qzeros, L0_ffn_down_g_idx)
    return x

_drawn_inputs = setup_inputs


def setup_inputs(seed=0):
    import zlib

    import numpy as np

    out = dict(_drawn_inputs(seed))
    spreads = {}
    factors = {}
    for name, (base, spread) in spreads.items():
        noise = np.random.default_rng([zlib.crc32(name.encode()), seed]).standard_normal(out[name].shape)
        drawn = base * np.exp(spread * noise) if base else spread * noise
        out[name] = jnp.asarray(drawn.astype(out[name].dtype))
    for name, factor in factors.items():
        out[name] = (out[name] * factor).astype(out[name].dtype)
    return out
```

```python
from contextlib import ExitStack

import concourse.bass as bass
from concourse import mybir
from concourse.alu_op_type import AluOpType as ALU

ACT = mybir.ActivationFunctionType
F32 = mybir.dt.float32
F16 = mybir.dt.float16
BF16 = mybir.dt.bfloat16
I32 = mybir.dt.int32
U8 = mybir.dt.uint8
AX_X = mybir.AxisListType.X
ABSMAX = bass.bass_isa.ReduceOp.absmax

P = 128
XBITS = 10
WBITS = 10
KBITS = -33
FLOOR = 2.0 ** -30
EPS = 1e-5


def at(start, size=1):
    return bass.ds(start, size)


def flat(ap):
    names = [f"d{n}" for n in range(len(ap.shape) - 1)]
    return ap.rearrange(f"p {' '.join(names)} -> p ({' '.join(names)})") if len(names) > 1 else ap


def wait_if(eng, semaphore, value):
    if not isinstance(value, int) or value > 0:
        eng.wait_ge(semaphore, value)


def run_first(eng, body):
    body(0, 0)
    body(1, 1)
    with eng.Fori(1, 4) as j:
        for u in range(2):
            body(2 * j + u, u)
    for i in range(8, 11):
        body(i, i % 2)


def run_second(eng, body):
    with eng.Fori(0, 5) as j:
        for u in range(2):
            body(2 * j + u, u)
    body(10, 0)


def flamingo_gated_block(nc, x, ctx_in, g_xattn, g_ffn, gate_q, gate_s, gate_z, gate_i,
                         up_q, up_s, up_z, up_i, down_q, down_s, down_z, down_i, out):
    B, S, D = x.shape
    INTER = gate_q.shape[1]
    GI, GD = gate_s.shape[0], down_s.shape[0]
    KT = D // P
    NT = -(-INTER // P)
    NPAD = NT * P
    HALF = B * S // 2
    BH = HALF // S
    LASTK = INTER - (NT - 1) * P
    TABLE = 2 * NPAD + D
    SCALE = float(S) ** -0.5
    assert S == P and D == 512 and HALF == 512 and KT == 4 and NT == 11 and GD <= 32

    with ExitStack() as stack:
        def sb(name, shape, dt):
            return stack.enter_context(nc.sbuf_tensor(name, shape, dt))

        def sem(name):
            return stack.enter_context(nc.semaphore(name))

        EARLY = B * D + 4 * 2 * D
        shared = sb("shared", [P, EARLY + TABLE], F32)
        ctx_sb = shared[:, 0:B * D].rearrange("p (b d) -> p b d", b=B)
        early = [shared[:, (B + 2 * n) * D:(B + 2 * n + 2) * D].rearrange("p (u d) -> p u d", u=2) for n in range(4)]
        query, ctxT, queryT, normed = early
        scale_rows = shared[:, EARLY:EARLY + TABLE]
        hidden = shared[:, 0:NT * B * S].bitcast(F16).rearrange("p (a i m) -> p a i m", a=2, i=NT)
        h_hi, h_lo = hidden[:, 0], hidden[:, 1]

        x_sb = sb("x_sb", [P, B, D], F32)
        nT_hi = sb("nT_hi", [P, KT, B * S], F16)
        nT_lo = sb("nT_lo", [P, KT, B * S], F16)
        qw = sb("qw", [P, 2, NPAD], I32)
        qd = sb("qd", [P, NT, D], I32)
        wd = qd[:, :, :].bitcast(F16).rearrange("p i (a n) -> p i a n", a=2)
        w_hi = sb("w_hi", [P, NT, 2, KT * P], F16)
        w_lo = sb("w_lo", [P, NT, 2, KT * P], F16)
        table = sb("table", [P, TABLE], BF16)
        ZW = (2 * INTER + D) // 8
        zq = sb("zq", [P, ZW], I32)
        z8 = sb("z8", [P, TABLE], U8)
        oh_s = sb("oh_s", [P, 2 * D + NPAD], BF16)
        oh_z = sb("oh_z", [P, 2 * D + NPAD], BF16)
        work = sb("work", [P, 10 * D], F32)
        IDX = 2 * D + INTER
        idx_i = work[:, 0:IDX].bitcast(I32)
        idx_f = work[:, 5 * D:5 * D + IDX]
        w_f32 = work[:, 0:4 * D].rearrange("p (u n) -> p u n", u=2)
        diff = work[:, 4 * D:6 * D]
        silu = work[:, 6 * D:8 * D].rearrange("p (u n) -> p u n", u=2)
        h_f32 = work[:, 8 * D:10 * D].rearrange("p (u n) -> p u n", u=2)
        probs = sb("probs", [P, 2, P], F32)
        ident = sb("ident", [P, P], F32)
        scale_flat = sb("scale_flat", [P, 2 * GI * INTER // P + GD * D // P], F32)
        lane = sb("lane", [P, 4], I32)
        pick = sb("pick", [P, 2], F32)
        half_pow = sb("half_pow", [P, 1], F32)
        gates = sb("gates", [P, 2], F32)
        tanhs = sb("tanhs", [P, 2], F32)
        top = sb("top", [P, 8], F32)
        top2 = sb("top2", [P, 16], F32)
        exp2 = top2[:, 0:3]
        inv2 = top2[:, 3:6]
        c_w = top2[:, 6:9]
        kappa = top2[:, 9:10]
        silu_scale = top2[:, 10:11]
        tau_a = top2[:, 11:12]
        tau = top2[:, 12:13]
        stats = sb("stats", [P, 2, B, 6], F32)
        mv = sb("mv", [P, 2, B, 2], F32)
        veps = sb("veps", [P, 2, B], F32)
        rstd = sb("rstd", [P, 2, B], F32)
        smax = sb("smax", [P, 4, B], F32)

        psum = stack.enter_context(nc.psum_tensor("psum", [P, 8, 512], F32))
        ctxT_ps = [psum[:, 0], psum[:, 1]]
        queryT_ps = [psum[:, 2], psum[:, 3]]
        score_ps = psum[:, 4, 0:P]
        value_ps = psum[:, 5]
        nT_ps = [psum[:, 6], psum[:, 7]]
        s_ps, z_ps = psum[:, 0:2], psum[:, 2:4]
        gate_ps = [psum[:, 4], psum[:, 5]]
        up_ps = [psum[:, 6], psum[:, 7]]
        sd_ps, zd_ps = psum[:, 0], psum[:, 2]

        x_in = [sem(f"x_in{b}") for b in range(B)]
        ctx_loaded = [sem(f"ctx_loaded{b}") for b in range(B)]
        gates_in, flat_in, rows_in, zeros_in, idx_in = (sem(n) for n in ("gates_in", "flat_in", "rows_in", "zeros_in", "idx_in"))
        qw_in, qd_in = sem("qw_in"), sem("qd_in")
        const_made, ident_made, rows_cleared = sem("const_made"), sem("ident_made"), sem("rows_cleared")
        lane_made = sem("lane_made")
        stats_made, mv_made, veps_made, rstd_made = sem("stats_made"), sem("mv_made"), sem("veps_made"), sem("rstd_made")
        normed_made, query_made = sem("normed_made"), sem("query_made")
        turned, turned_copied = sem("turned"), sem("turned_copied")
        scored, max_made, bias_made, exp_made = sem("scored"), sem("max_made"), sem("bias_made"), sem("exp_made")
        inv_made, probs_made, valued, x2_made = sem("inv_made"), sem("probs_made"), sem("valued"), sem("x2_made")
        n_turned, n_hi_made, n_lo_made = sem("n_turned"), sem("n_hi_made"), sem("n_lo_made")
        split_step, zeros_step, zeros_made = sem("split_step"), sem("zeros_step"), sem("zeros_made")
        idx_step, onehot_made = sem("idx_step"), sem("onehot_made")
        qw_unpacked, qd_unpacked = sem("qw_unpacked"), sem("qd_unpacked")
        own_top, all_top, scalar_step, scalars_made, tanh_made = (sem(n) for n in ("own_top", "all_top", "scalar_step", "scalars_made", "tanh_made"))
        gathered, diff_made, w_formed, w_hi_made, w_lo_made = (sem(n) for n in ("gathered", "diff_made", "w_formed", "w_hi_made", "w_lo_made"))
        acc_ready, silu_made, h_formed, h_hi_made, h_lo_made = (sem(n) for n in ("acc_ready", "silu_made", "h_formed", "h_hi_made", "h_lo_made"))
        down_ready, out_formed, stored = sem("down_ready"), sem("out_formed"), sem("stored")

        block = stack.enter_context(nc.Block())

        def column(vec, lo, n):
            return bass.AP(tensor=vec.tensor, offset=vec.offset + lo, ap=[[0, P], [1, n]])

        ln_order = [(0, 0), (0, 1)]
        for s in range(B + 2):
            ln_order += [(0, s + 2)] * (s + 2 < B) + [(1, s - 1)] * (0 <= s - 1 < B)
        mv_count = {key: n + 1 for n, key in enumerate(ln_order)}

        @block.sync
        def _(sp):
            for b in range(B):
                sp.dma_start(x_sb[:, b, :], x[b]).then_inc(x_in[b], 16)
                sp.dma_start(ctx_sb[:, b, :], ctx_in[b]).then_inc(ctx_loaded[b], 16)
                if b == 1:
                    for h in range(2):
                        sp.dma_start(qw[64 * h:64 * h + 64, 0, 0:INTER], gate_q).then_inc(qw_in, 16)
                        sp.dma_start(qw[64 * h:64 * h + 64, 1, 0:INTER], up_q).then_inc(qw_in, 16)
            for i in range(NT):
                rows = min(P, INTER - i * P) // 8
                src = bass.AP(tensor=down_q.tensor, offset=down_q.offset + 16 * i * D, ap=[[D, rows], [0, 8], [1, D]])
                if i == NT - 1:
                    sp.wait_ge(rows_cleared, 2)
                sp.dma_start(qd[0:8 * rows, i, :], src).then_inc(qd_in, 16)
            with sp.Fori(0, B) as m:
                sp.wait_ge(out_formed, m + 1)
                sp.dma_start(out[bass.ds(m, 1)].rearrange("a s d -> (a s) d"), x_sb[:, bass.ds(m, 1), :].rearrange("p a d -> p (a d)")).then_inc(stored, 16)
            sp.wait_ge(stored, 16 * B)

        @block.gpsimd
        def _(pool):
            pool.memset(scale_rows, 0.0).then_inc(rows_cleared, 1)
            pool.memset(qd[:, NT - 1, :], 0).then_inc(rows_cleared, 1)
            pool.memset(ident[:, :], 0.0).then_inc(ident_made, 1)
            pool.wait_ge(ident_made, 1)
            pool.affine_select(out=ident[:, :], in_=ident[:, :], compare_op=ALU.not_equal, fill=1.0, base=0,
                               pattern=[[-1, P]], channel_multiplier=1).then_inc(ident_made, 1)
            pool.memset(qw[:, :, INTER:NPAD], 0).then_inc(rows_cleared, 1)
            pool.iota(lane[:, 0:1], pattern=[[0, 1]], base=0, channel_multiplier=1).then_inc(const_made, 1)
            pool.memset(half_pow[:, :], -0.5).then_inc(const_made, 1)

            def tables():
                n = 0
                for lo, hi in ((0, NPAD), (NPAD, 2 * NPAD), (2 * NPAD, TABLE)):
                    yield lambda lo=lo, hi=hi: pool.tensor_copy(table[:, lo:hi], scale_rows[:, lo:hi])
                    yield lambda lo=lo, hi=hi: pool.tensor_tensor(scale_rows[64:P, lo:hi], scale_rows[64:P, lo:hi], table[64:P, lo:hi], ALU.subtract)
                    yield lambda lo=lo, hi=hi: pool.tensor_copy(table[64:P, lo:hi], scale_rows[64:P, lo:hi])
                    yield lambda lo=lo, hi=hi: pool.tensor_tensor(table[96:P, lo:hi], scale_rows[96:P, lo:hi], table[96:P, lo:hi], ALU.subtract)

            def rstds(ln, b):
                pool.wait_ge(mv_made, mv_count[ln, b])
                pool.tensor_scalar(veps[:, ln, b:b + 1], mv[:, ln, b, 1:2], EPS, None, ALU.add).then_inc(veps_made, 1)
                pool.wait_ge(veps_made, mv_count[ln, b])
                pool.tensor_tensor(rstd[:, ln, b:b + 1], veps[:, ln, b:b + 1], half_pow[:, :], ALU.pow).then_inc(rstd_made, 1)

            pieces = list(tables())
            done = 0
            for n, (ln, b) in enumerate(ln_order):
                if n == 0:
                    pool.wait_ge(const_made, 2)
                rstds(ln, b)
                if n == 3:
                    pool.wait_ge(rows_in, 16 * 9)
                    pool.wait_ge(own_top, 3)
                    pool.partition_all_reduce(top[:, 3:6], top[:, 0:3], P, ABSMAX).then_inc(all_top, 1)
                if n >= 3 and done < len(pieces):
                    pool.wait_ge(rstd_made, n + 1)
                    pieces[done]().then_inc(split_step, 1)
                    done += 1
                    pool.wait_ge(split_step, done)
            assert done == len(pieces)

            def low_w_gate_up(i, u):
                pool.wait_ge(w_hi_made, i + 1)
                pool.tensor_tensor(w_lo[:, at(i), :, :].rearrange("p a t n -> p (a t n)"), w_f32[:, u, :],
                                   w_hi[:, at(i), :, :].rearrange("p a t n -> p (a t n)"), ALU.subtract).then_inc(w_lo_made, 1)

            def low_w_down(i, u):
                pool.wait_ge(w_hi_made, NT + i + 1)
                pool.tensor_tensor(flat(wd[:, at(i), 1]), w_f32[:, u, 0:D], flat(wd[:, at(i), 0]), ALU.subtract).then_inc(w_lo_made, 1)

            def low_h(half, i, u):
                n = half * NT + i
                pool.wait_ge(h_hi_made, n + 1)
                pool.tensor_tensor(flat(h_lo[:, at(i), half * HALF:(half + 1) * HALF]), h_f32[:, u, :],
                                   flat(h_hi[:, at(i), half * HALF:(half + 1) * HALF]), ALU.subtract).then_inc(h_lo_made, 1)

            def first_half(i, u):
                if not isinstance(i, int) or i + 2 < NT:
                    low_w_gate_up(i + 2, u)
                low_h(0, i, u)

            def second_half(i, u):
                low_w_down(i, u ^ 1)
                low_h(1, i, u ^ 1)

            low_w_gate_up(0, 0)
            low_w_gate_up(1, 1)
            run_first(pool, first_half)
            run_second(pool, second_half)

        @block.vector
        def _(dve):
            def ln_stats(ln, b):
                n = mv_count[ln, b]
                if ln == 0:
                    dve.wait_ge(x_in[b], 16)
                else:
                    dve.wait_ge(x2_made, b + 1)
                dve.bn_stats(stats[:, ln, b, :], x_sb[:, b, :]).then_inc(stats_made, 1)
                dve.wait_ge(stats_made, n)
                dve.bn_aggr(mv[:, ln, b, :], stats[:, ln, b, :]).then_inc(mv_made, 1)

            def make_query(b):
                dve.wait_ge(rstd_made, mv_count[0, b])
                if b >= 2:
                    dve.wait_ge(turned, b - 1)
                dve.tensor_scalar(query[:, b % 2, :], x_sb[:, b, :], mv[:, 0, b, 0:1], rstd[:, 0, b:b + 1],
                                  ALU.subtract, ALU.mult).then_inc(query_made, 1)

            def score_max(b):
                dve.wait_ge(scored, b + 1)
                dve.tensor_reduce(smax[:, 0, b:b + 1], score_ps, AX_X, ALU.max, negate=True).then_inc(max_made, 1)
                dve.wait_ge(max_made, b + 1)
                dve.tensor_scalar(smax[:, 1, b:b + 1], smax[:, 0, b:b + 1], SCALE, None, ALU.mult).then_inc(bias_made, 1)

            def normalise(b):
                dve.wait_ge(exp_made, b + 1)
                dve.reciprocal(smax[:, 3, b:b + 1], smax[:, 2, b:b + 1]).then_inc(inv_made, 1)
                dve.wait_ge(inv_made, b + 1)
                dve.tensor_scalar(probs[:, b % 2, :], probs[:, b % 2, :], smax[:, 3, b:b + 1], None, ALU.mult).then_inc(probs_made, 1)

            def residual(b):
                dve.wait_ge(valued, b + 1)
                if b == 0:
                    dve.wait_ge(tanh_made, 1)
                dve.wait_ge(query_made, b + 1)
                dve.scalar_tensor_tensor(out=x_sb[:, b, :], in0=value_ps, scalar=tanhs[:, 0:1], in1=x_sb[:, b, :],
                                         op0=ALU.mult, op1=ALU.add).then_inc(x2_made, 1)

            def make_normed(b):
                dve.wait_ge(rstd_made, mv_count[1, b])
                if b >= 2:
                    dve.wait_ge(n_turned, b - 1)
                dve.tensor_scalar(normed[:, b % 2, :].rearrange("p (t h r) -> p t h r", t=KT, h=2),
                                  x_sb[:, b, :].rearrange("p (r t h) -> p t h r", t=KT, h=2), mv[:, 1, b, 0:1], rstd[:, 1, b:b + 1],
                                  ALU.subtract, ALU.mult).then_inc(normed_made, 1)

            def n_low(b):
                dve.wait_ge(n_hi_made, b + 1)
                dve.scalar_tensor_tensor(out=nT_lo[:, :, b * S:(b + 1) * S], in0=nT_ps[b % 2].rearrange("p (t m) -> p t m", t=KT),
                                         scalar=2.0 ** XBITS, in1=nT_hi[:, :, b * S:(b + 1) * S],
                                         op0=ALU.mult, op1=ALU.subtract).then_inc(n_lo_made, 1)

            def lanes():
                dve.wait_ge(const_made, 1)
                dve.tensor_scalar(lane[:, 1:2], lane[:, 0:1], 31, None, ALU.bitwise_and).then_inc(lane_made, 1)
                dve.tensor_scalar(lane[:, 2:3], lane[:, 0:1], 7, 2, ALU.bitwise_and, ALU.logical_shift_left).then_inc(lane_made, 1)
                dve.memset(pick[:, 1:2], -1.0).then_inc(lane_made, 1)
                dve.memset(lane[:, 3:4], 15).then_inc(lane_made, 1)
                dve.wait_ge(lane_made, 4)
                dve.tensor_copy(pick[:, 0:1], lane[:, 1:2]).then_inc(lane_made, 1)
                dve.tensor_copy(pick[32:64, 1:2], lane[32:64, 1:2]).then_inc(lane_made, 1)
                dve.wait_ge(lane_made, 6)
                dve.memset(pick[32:64, 0:1], -1.0).then_inc(lane_made, 1)

            def own_tops():
                dve.wait_ge(flat_in, 48)
                a, bb = GI * INTER // P, 2 * GI * INTER // P
                for n, (lo, hi) in enumerate(((0, a), (a, bb), (bb, bb + GD * D // P))):
                    dve.tensor_reduce(top[:, n:n + 1], scale_flat[:, lo:hi], AX_X, ALU.max,
                                      apply_absolute_value=True).then_inc(own_top, 1)

            def scalars():
                dve.wait_ge(all_top, 1)
                dve.tensor_scalar(top[:, 3:6], top[:, 3:6], FLOOR, None, ALU.max).then_inc(scalar_step, 1)
                dve.wait_ge(scalar_step, 1)
                dve.tensor_scalar(exp2.bitcast(I32), top[:, 3:6].bitcast(I32), 0x7F800000, None, ALU.bitwise_and).then_inc(scalar_step, 1)
                dve.wait_ge(scalar_step, 2)
                dve.reciprocal(inv2, exp2).then_inc(scalar_step, 1)
                dve.wait_ge(scalar_step, 3)
                dve.tensor_scalar(c_w, inv2, 2.0 ** WBITS, None, ALU.mult).then_inc(scalars_made, 1)
                dve.tensor_scalar(kappa, inv2[:, 0:1], 2.0 ** KBITS, None, ALU.mult).then_inc(scalars_made, 1)
                dve.tensor_scalar(silu_scale, exp2[:, 0:1], 2.0 ** -(XBITS + WBITS), None, ALU.mult).then_inc(scalars_made, 1)
                dve.scalar_tensor_tensor(out=tau_a, in0=exp2[:, 0:1], scalar=2.0 ** -(XBITS + 2 * WBITS + KBITS), in1=exp2[:, 1:2],
                                         op0=ALU.mult, op1=ALU.mult).then_inc(scalar_step, 1)
                dve.wait_ge(scalar_step, 4)
                dve.wait_ge(tanh_made, 1)
                dve.scalar_tensor_tensor(out=tau, in0=tau_a, scalar=exp2[:, 2:3], in1=tanhs[:, 1:2],
                                         op0=ALU.mult, op1=ALU.mult).then_inc(scalars_made, 1)

            def unpack_gate_up():
                dve.wait_ge(qw_in, 64)
                dve.wait_ge(rows_cleared, 3)
                dve.tensor_scalar(qw[0:64, :, :], qw[0:64, :, :], 0x0F0F0F0F, None, ALU.bitwise_and).then_inc(qw_unpacked, 1)
                dve.tensor_scalar(qw[64:P, :, :], qw[64:P, :, :], 4, 0x0F0F0F0F, ALU.logical_shift_right, ALU.bitwise_and).then_inc(qw_unpacked, 1)

            def zeros():
                dve.wait_ge(zeros_in, 48)
                zb = zq[:, :].bitcast(U8)
                two = z8[:, 0:2 * NPAD].rearrange("p (a n) -> p a n", a=2)[:, :, 0:INTER].rearrange("p a (b h) -> p a b h", h=2)
                one = z8[:, 2 * NPAD:TABLE].rearrange("p (b h) -> p b h", h=2)
                for h in range(2):
                    dve.tensor_scalar(two[32:32 + GI, :, :, h], zb[32:32 + GI, 0:INTER].rearrange("p (a b) -> p a b", a=2),
                                      4 * h, 15, ALU.logical_shift_right, ALU.bitwise_and).then_inc(zeros_step, 1)
                    dve.tensor_scalar(one[32:32 + GD, :, h], zb[32:32 + GD, INTER:INTER + D // 2],
                                      4 * h, 15, ALU.logical_shift_right, ALU.bitwise_and).then_inc(zeros_step, 1)
                dve.wait_ge(zeros_step, 4)
                dve.wait_ge(split_step, 12)
                for tb in range(2):
                    dve.tensor_scalar(table[32:32 + GI, tb * NPAD:tb * NPAD + INTER], z8[32:32 + GI, tb * NPAD:tb * NPAD + INTER],
                                      1.0, None, ALU.add).then_inc(zeros_made, 1)
                dve.tensor_scalar(table[32:32 + GD, 2 * NPAD:TABLE], z8[32:32 + GD, 2 * NPAD:TABLE], 1.0, None, ALU.add).then_inc(zeros_made, 1)

            def indices(part):
                lo, hi, groups = ((0, 2 * D, GI), (2 * D, IDX, GD))[part]
                dve.wait_ge(idx_in, 48)
                dve.tensor_scalar(idx_f[:, lo:hi], idx_i[:, lo:hi], 0.0, float(groups), ALU.is_lt, ALU.mult).then_inc(idx_step, 1)
                dve.wait_ge(idx_step, 3 * part + 1)
                dve.tensor_tensor(idx_f[:, lo:hi], idx_i[:, lo:hi], idx_f[:, lo:hi], ALU.add).then_inc(idx_step, 1)
                dve.wait_ge(idx_step, 3 * part + 2)
                dve.tensor_scalar(idx_f[:, lo:hi], idx_f[:, lo:hi], 0.0, float(groups - 1), ALU.max, ALU.min).then_inc(idx_step, 1)

            def onehots(part):
                dve.wait_ge(idx_step, 3 * part + 3)
                dve.wait_ge(lane_made, 7)
                for n, oh in enumerate((oh_s, oh_z)):
                    if part == 0:
                        for tb in range(2):
                            dve.tensor_scalar(oh[:, tb * D:(tb + 1) * D].rearrange("p (t h r) -> p t h r", t=KT, h=2),
                                              idx_f[:, tb * D:(tb + 1) * D].rearrange("p (r t h) -> p t h r", t=KT, h=2),
                                              pick[:, n:n + 1], None, ALU.is_equal).then_inc(onehot_made, 1)
                    else:
                        dve.memset(oh[:, IDX:2 * D + NPAD], 0.0).then_inc(onehot_made, 1)
                        dve.tensor_scalar(oh[:, 2 * D:IDX], idx_f[:, 2 * D:IDX], pick[:, n:n + 1], None, ALU.is_equal).then_inc(onehot_made, 1)

            extras = {0: [lanes, own_tops], 1: [unpack_gate_up], 2: [lambda: indices(0), scalars], 3: [lambda: onehots(0)],
                      4: [lambda: indices(1)], 5: [lambda: onehots(1)], 8: [zeros]}

            ln_stats(0, 0)
            ln_stats(0, 1)
            make_query(0)
            make_query(1)
            for s in range(B + 2):
                if s + 2 < B:
                    ln_stats(0, s + 2)
                if s < B:
                    score_max(s)
                if 0 <= s - 1 < B:
                    residual(s - 1)
                    ln_stats(1, s - 1)
                if s < B:
                    normalise(s)
                if s + 2 < B:
                    make_query(s + 2)
                if 0 <= s - 2 < B:
                    n_low(s - 2)
                if 0 <= s - 1 < B:
                    make_normed(s - 1)
                for piece in extras.get(s, []):
                    piece()

            def dequant_gate_up(i, u):
                dve.wait_ge(gathered, i + 1)
                wait_if(dve, w_formed, 2 * i)
                for tb in range(2):
                    nib = qw[:, tb, :].bitcast(U8)
                    dve.tensor_tensor(diff[:, tb * D:(tb + 1) * D].rearrange("p (t n) -> p t n", t=KT),
                                      nib.rearrange("p (n t) -> p t n", t=KT)[:, :, at(i * P, P)], z_ps[:, tb, :].rearrange("p (t n) -> p t n", t=KT),
                                      ALU.subtract).then_inc(diff_made, 1)
                for tb in range(2):
                    dve.wait_ge(diff_made, 2 * i + tb + 1)
                    wait_if(dve, w_lo_made, i - 1)
                    dve.scalar_tensor_tensor(out=w_f32[:, u, tb * D:(tb + 1) * D], in0=diff[:, tb * D:(tb + 1) * D], scalar=c_w[:, tb:tb + 1],
                                             in1=s_ps[:, tb, :], op0=ALU.mult, op1=ALU.mult).then_inc(w_formed, 1)

            def dequant_down(i, u):
                dve.wait_ge(gathered, NT + i + 1)
                dve.wait_ge(w_formed, 2 * NT + i)
                dve.tensor_tensor(diff[:, 0:D], flat(qd[:, at(i), :]), zd_ps, ALU.subtract).then_inc(diff_made, 1)
                dve.wait_ge(diff_made, 2 * NT + i + 1)
                dve.wait_ge(w_lo_made, NT + i - 1)
                dve.scalar_tensor_tensor(out=w_f32[:, u, 0:D], in0=diff[:, 0:D], scalar=c_w[:, 2:3], in1=sd_ps,
                                         op0=ALU.mult, op1=ALU.mult).then_inc(w_formed, 1)

            def form_hidden(n, u):
                dve.wait_ge(silu_made, n + 1)
                wait_if(dve, h_lo_made, n - 1)
                dve.scalar_tensor_tensor(out=h_f32[:, u, :], in0=silu[:, u, :], scalar=kappa, in1=up_ps[u],
                                         op0=ALU.mult, op1=ALU.mult).then_inc(h_formed, 1)

            def first_half(i, u):
                if not isinstance(i, int) or i + 2 < NT:
                    dequant_gate_up(i + 2, u)
                form_hidden(i, u)

            def second_half(i, u):
                dequant_down(i, u ^ 1)
                form_hidden(NT + i, u ^ 1)

            dve.wait_ge(qw_unpacked, 2)
            dve.wait_ge(scalars_made, 4)
            dve.wait_ge(onehot_made, 8)
            dequant_gate_up(0, 0)
            dequant_gate_up(1, 1)
            run_first(dve, first_half)
            dve.wait_ge(qd_in, 16 * NT)
            dve.tensor_scalar(qd[:, :, :], qd[:, :, :], lane[:, 2:3], lane[:, 3:4], ALU.logical_shift_right, ALU.bitwise_and).then_inc(qd_unpacked, 1)
            dve.wait_ge(qd_unpacked, 1)
            run_second(dve, second_half)

            with dve.Fori(0, B) as m:
                dve.wait_ge(down_ready, m + 1)
                row = flat(x_sb[:, at(m), :])
                dve.scalar_tensor_tensor(out=row, in0=flat(psum[:, at(m), :]), scalar=tau, in1=row,
                                         op0=ALU.mult, op1=ALU.add).then_inc(out_formed, 1)

        @block.scalar
        def _(act):
            act.dma_start(gates[:, 0:1], column(g_xattn, 0, 1)).then_inc(gates_in, 16)
            act.dma_start(gates[:, 1:2], column(g_ffn, 0, 1)).then_inc(gates_in, 16)
            a = GI * INTER // P
            act.dma_start(scale_flat[:, 0:a], gate_s.rearrange("g n -> (g n)").rearrange("(p c) -> p c", p=P)).then_inc(flat_in, 16)
            act.dma_start(scale_flat[:, a:2 * a], up_s.rearrange("g n -> (g n)").rearrange("(p c) -> p c", p=P)).then_inc(flat_in, 16)
            act.dma_start(scale_flat[:, 2 * a:], down_s.rearrange("g n -> (g n)").rearrange("(p c) -> p c", p=P)).then_inc(flat_in, 16)
            act.dma_start(idx_i[:, 0:D], column(gate_i, 0, D)).then_inc(idx_in, 16)
            act.dma_start(idx_i[:, D:2 * D], column(up_i, 0, D)).then_inc(idx_in, 16)
            act.dma_start(idx_i[:, 2 * D:IDX], column(down_i, 0, INTER)).then_inc(idx_in, 16)
            act.dma_start(zq[32:32 + GI, 0:INTER // 8], gate_z).then_inc(zeros_in, 16)
            act.dma_start(zq[32:32 + GI, INTER // 8:2 * INTER // 8], up_z).then_inc(zeros_in, 16)
            act.dma_start(zq[32:32 + GD, 2 * INTER // 8:ZW], down_z).then_inc(zeros_in, 16)
            act.wait_ge(rows_cleared, 1)
            for r in (0, 64, 96):
                act.dma_start(scale_rows[r:r + GI, 0:INTER], gate_s).then_inc(rows_in, 16)
                act.dma_start(scale_rows[r:r + GI, NPAD:NPAD + INTER], up_s).then_inc(rows_in, 16)
                act.dma_start(scale_rows[r:r + GD, 2 * NPAD:TABLE], down_s).then_inc(rows_in, 16)
            act.wait_ge(gates_in, 32)
            act.activation(tanhs[:, :], gates[:, :], ACT.Tanh).then_inc(tanh_made, 1)

            def copies(b):
                act.wait_ge(turned, b + 1)
                if b >= 2:
                    act.wait_ge(scored, b - 1)
                act.activation(ctxT[:, b % 2, :], ctxT_ps[b % 2], ACT.Copy).then_inc(turned_copied, 1)
                act.activation(queryT[:, b % 2, :], queryT_ps[b % 2], ACT.Copy).then_inc(turned_copied, 1)

            def exponentials(b):
                act.wait_ge(bias_made, b + 1)
                if b >= 2:
                    act.wait_ge(valued, b - 1)
                act.activation(probs[:, b % 2, :], score_ps, ACT.Exp, bias=smax[:, 1, b:b + 1], scale=SCALE,
                               accum_out=smax[:, 2, b:b + 1]).then_inc(exp_made, 1)

            def n_high(b):
                act.wait_ge(n_turned, b + 1)
                act.activation(nT_hi[:, :, b * S:(b + 1) * S], nT_ps[b % 2].rearrange("p (t m) -> p t m", t=KT),
                               ACT.Copy, scale=2.0 ** XBITS).then_inc(n_hi_made, 1)

            copies(0)
            for s in range(B + 2):
                if s < B:
                    exponentials(s)
                if 0 <= s - 2:
                    n_high(s - 2)
                if s + 1 < B:
                    copies(s + 1)

            def high_w_gate_up(i, u):
                act.wait_ge(w_formed, 2 * i + 2)
                act.activation(w_hi[:, at(i), :, :].rearrange("p a t n -> p (a t n)"), w_f32[:, u, :], ACT.Copy).then_inc(w_hi_made, 1)

            def high_w_down(i, u):
                act.wait_ge(w_formed, 2 * NT + i + 1)
                act.activation(flat(wd[:, at(i), 0]), w_f32[:, u, 0:D], ACT.Copy).then_inc(w_hi_made, 1)

            def gate_silu(n, u):
                act.wait_ge(acc_ready, n + 1)
                wait_if(act, h_formed, n - 1)
                act.activation(silu[:, u, :], gate_ps[u], ACT.Silu, scale=silu_scale).then_inc(silu_made, 1)

            def high_h(half, i, u):
                act.wait_ge(h_formed, half * NT + i + 1)
                act.activation(flat(h_hi[:, at(i), half * HALF:(half + 1) * HALF]), h_f32[:, u, :], ACT.Copy).then_inc(h_hi_made, 1)

            def first_half(i, u):
                if not isinstance(i, int) or i + 2 < NT:
                    high_w_gate_up(i + 2, u)
                gate_silu(i, u)
                high_h(0, i, u)

            def second_half(i, u):
                high_w_down(i, u ^ 1)
                gate_silu(NT + i, u ^ 1)
                high_h(1, i, u ^ 1)

            high_w_gate_up(0, 0)
            high_w_gate_up(1, 1)
            act.wait_ge(scalars_made, 4)
            run_first(act, first_half)
            run_second(act, second_half)

        @block.tensor
        def _(pe):
            def turn(b):
                pe.wait_ge(ctx_loaded[b], 16)
                if b >= 2:
                    pe.wait_ge(turned_copied, 2 * (b - 1))
                for t in range(KT):
                    pe.transpose(ctxT_ps[b % 2][:, t * P:(t + 1) * P], ctx_sb[:, b, t * P:(t + 1) * P], ident[:, :])
                pe.wait_ge(query_made, b + 1)
                for t in range(KT):
                    mm = pe.transpose(queryT_ps[b % 2][:, t * P:(t + 1) * P], query[:, b % 2, t * P:(t + 1) * P], ident[:, :])
                mm.then_inc(turned, 1)

            def scores(b):
                pe.wait_ge(turned_copied, 2 * (b + 1))
                if b:
                    pe.wait_ge(exp_made, b)
                for t in range(KT):
                    mm = pe.matmul(score_ps, queryT[:, b % 2, t * P:(t + 1) * P], ctxT[:, b % 2, t * P:(t + 1) * P],
                                   start=(t == 0), stop=(t == KT - 1))
                mm.then_inc(scored, 1)

            def values(b):
                pe.wait_ge(probs_made, b + 1)
                if b:
                    pe.wait_ge(x2_made, b)
                pe.matmul(value_ps, probs[:, b % 2, :], ctx_sb[:, b, :], start=True, stop=True).then_inc(valued, 1)

            def turn_normed(b):
                pe.wait_ge(normed_made, b + 1)
                if b >= 2:
                    pe.wait_ge(n_lo_made, b - 1)
                for t in range(KT):
                    mm = pe.transpose(nT_ps[b % 2][:, t * P:(t + 1) * P], normed[:, b % 2, t * P:(t + 1) * P], ident[:, :])
                mm.then_inc(n_turned, 1)

            pe.wait_ge(ident_made, 2)
            turn(0)
            for s in range(B + 2):
                if s < B:
                    scores(s)
                if 0 <= s - 1 < B:
                    values(s - 1)
                if 0 <= s - 2:
                    turn_normed(s - 2)
                if s + 1 < B:
                    turn(s + 1)

            def gather_gate_up(i):
                wait_if(pe, w_formed, 2 * i)
                for tb in range(2):
                    cols = table[:, at(i * P + tb * NPAD, P)]
                    for t in range(KT):
                        k = slice(tb * D + t * P, tb * D + (t + 1) * P)
                        pe.matmul(s_ps[:, tb, t * P:(t + 1) * P], oh_s[:, k], cols, start=True, stop=True)
                        mm = pe.matmul(z_ps[:, tb, t * P:(t + 1) * P], oh_z[:, k], cols, start=True, stop=True)
                mm.then_inc(gathered, 1)

            def gather_down(i):
                pe.wait_ge(w_formed, 2 * NT + i)
                cols = table[:, 2 * NPAD:TABLE]
                k = at(i * P + 2 * D, P)
                pe.matmul(sd_ps, oh_s[:, k], cols, start=True, stop=True)
                pe.matmul(zd_ps, oh_z[:, k], cols, start=True, stop=True).then_inc(gathered, 1)

            def gate_up(half, i, u):
                n = half * NT + i
                if half == 0:
                    pe.wait_ge(w_lo_made, i + 1)
                wait_if(pe, h_formed, n - 1)
                tok = slice(half * HALF, (half + 1) * HALF)
                for tb, acc in enumerate((gate_ps[u], up_ps[u])):
                    for t in range(KT):
                        hi = flat(w_hi[:, at(i), tb, t * P:(t + 1) * P])
                        lo = flat(w_lo[:, at(i), tb, t * P:(t + 1) * P])
                        pe.matmul(acc, hi, nT_hi[:, t, tok], start=(t == 0), stop=False)
                        pe.matmul(acc, hi, nT_lo[:, t, tok], start=False, stop=False)
                        mm = pe.matmul(acc, lo, nT_hi[:, t, tok], start=False, stop=(t == KT - 1))
                mm.then_inc(acc_ready, 1)

            def first_half(i, u):
                if not isinstance(i, int) or i + 2 < NT:
                    gather_gate_up(i + 2)
                gate_up(0, i, u)

            def second_half(i, u):
                gather_down(i)
                gate_up(1, i, u ^ 1)

            pe.wait_ge(onehot_made, 8)
            pe.wait_ge(zeros_made, 3)
            pe.wait_ge(turned_copied, 2 * B)
            gather_gate_up(0)
            gather_gate_up(1)
            pe.wait_ge(n_lo_made, B)
            run_first(pe, first_half)
            run_second(pe, second_half)

            pe.wait_ge(w_lo_made, 2 * NT)
            for half in range(2):
                pe.wait_ge(h_lo_made, (half + 1) * NT)
                with pe.Fori(half * BH, (half + 1) * BH) as m:
                    acc = flat(psum[:, at(m), :])
                    for i in range(NT):
                        hi = flat(h_hi[:, i:i + 1, at(m * P, P)])
                        lo = flat(h_lo[:, i:i + 1, at(m * P, P)])
                        pe.matmul(acc, hi, wd[:, i, 0], start=(i == 0), stop=False)
                        pe.matmul(acc, hi, wd[:, i, 1], start=False, stop=False)
                        mm = pe.matmul(acc, lo, wd[:, i, 0], start=False, stop=(i == NT - 1))
                    mm.then_inc(down_ready, 1)


_INS = ["x", "ctx_4096", "g_xattn", "g_ffn"] + [f"L0_ffn_{m}_{part}" for m in ("gate", "up", "down")
                                                 for part in ("qweight", "scales", "qzeros", "g_idx")]
_OUTS = [((8, 128, 512), "float32")]


def kernel(**inputs):
    import numpy as _np
    import concourse.bacc as _bacc
    from concourse import mybir as _mybir
    from concourse.bass_utils import run_bass_kernel_spmd as _run

    nc = _bacc.Bacc("TRN2", target_bir_lowering=False, num_devices=1)
    arrays, args = {}, []
    for name in _INS:
        a = _np.ascontiguousarray(inputs[name])
        arrays[f"in_{name}_dram"] = a
        args.append(nc.dram_tensor(f"in_{name}_dram", a.shape, _mybir.dt.from_np(a.dtype), kind="ExternalInput").ap())
    for n, (shape, dtype) in enumerate(_OUTS):
        dt = _mybir.dt.from_np(_np.dtype(dtype))
        args.append(nc.dram_tensor(f"out_{n}_dram", shape, dt, kind="ExternalOutput").ap())
    flamingo_gated_block(nc, *args)
    r = _run(nc, [arrays], core_ids=[0])
    return r.results[0]["out_0_dram"]
```

```python
from contextlib import ExitStack

import concourse.bass as bass
from concourse import mybir
from concourse.alu_op_type import AluOpType as ALU

ACT = mybir.ActivationFunctionType
F32 = mybir.dt.float32
F16 = mybir.dt.float16
BF16 = mybir.dt.bfloat16
I32 = mybir.dt.int32
U8 = mybir.dt.uint8
AX_X = mybir.AxisListType.X
ABSMAX = bass.bass_isa.ReduceOp.absmax

P = 128
XBITS = 10
WBITS = 10
KBITS = -33
FLOOR = 2.0 ** -30
EPS = 1e-5
FIRST_MIXED = 6


def at(start, size=1):
    return bass.ds(start, size)


def flat(ap):
    names = [f"d{n}" for n in range(len(ap.shape) - 1)]
    return ap.rearrange(f"p {' '.join(names)} -> p ({' '.join(names)})") if len(names) > 1 else ap


def wait_if(eng, semaphore, value):
    if not isinstance(value, int) or value > 0:
        eng.wait_ge(semaphore, value)


def run_first(eng, tile, attention_step):
    for i in range(5):
        tile(i, i % 2)
        attention_step(FIRST_MIXED + i)
    with eng.Fori(0, 2) as j:
        for u in range(2):
            tile(2 * j + u + 5, 1 - u)
    for i in range(9, 11):
        tile(i, i % 2)


def run_second(eng, tile):
    with eng.Fori(0, 5) as j:
        for u in range(2):
            tile(2 * j + u, 1 - u)
    tile(10, 1)


def flamingo_gated_block(nc, x, ctx_in, g_xattn, g_ffn, gate_q, gate_s, gate_z, gate_i,
                         up_q, up_s, up_z, up_i, down_q, down_s, down_z, down_i, out):
    B, S, D = x.shape
    INTER = gate_q.shape[1]
    GI, GD = gate_s.shape[0], down_s.shape[0]
    KT = D // P
    NT = -(-INTER // P)
    NPAD = NT * P
    HALF = B * S // 2
    BH = HALF // S
    LASTK = INTER - (NT - 1) * P
    TABLE = 2 * NPAD + D
    SCALE = float(S) ** -0.5
    assert S == P and D == 512 and HALF == 512 and KT == 4 and NT == 11 and GD <= 32

    with ExitStack() as stack:
        def sb(name, shape, dt):
            return stack.enter_context(nc.sbuf_tensor(name, shape, dt))

        def sem(name):
            return stack.enter_context(nc.semaphore(name))

        EARLY = B * D + 4 * 2 * D
        shared = sb("shared", [P, EARLY + TABLE], F32)
        ctx_sb = shared[:, 0:B * D].rearrange("p (b d) -> p b d", b=B)
        early = [shared[:, (B + 2 * n) * D:(B + 2 * n + 2) * D].rearrange("p (u d) -> p u d", u=2) for n in range(4)]
        query, ctxT, queryT, normed = early
        scale_rows = shared[:, EARLY:EARLY + TABLE]
        hidden = shared[:, 0:NT * B * S].bitcast(F16).rearrange("p (h i a m) -> p h i a m", h=2, i=NT, a=2)

        x_sb = sb("x_sb", [P, B, D], F32)
        nT_hi = sb("nT_hi", [P, KT, B * S], F16)
        nT_lo = sb("nT_lo", [P, KT, B * S], F16)
        qw = sb("qw", [P, 2, NPAD], I32)
        qd = sb("qd", [P, NT, D], I32)
        wd = qd[:, :, :].bitcast(F16).rearrange("p i (a n) -> p i a n", a=2)
        w_hi = sb("w_hi", [P, NT, 2, KT * P], F16)
        w_lo = sb("w_lo", [P, NT, 2, KT * P], F16)
        table_s = sb("table_s", [P, TABLE], BF16)
        table_z = sb("table_z", [32, TABLE], BF16)
        ZW = (2 * INTER + D) // 8
        zq = sb("zq", [P, ZW], I32)
        z8 = sb("z8", [P, TABLE], U8)
        onehot = sb("onehot", [P, 2 * D + NPAD], BF16)
        work = sb("work", [P, 10 * D], F32)
        idx_i = [work[:, 0:2 * D].bitcast(I32), scale_rows[:, 0:INTER].bitcast(I32)]
        idx_f = [work[:, 2 * D:4 * D], scale_rows[:, INTER:2 * INTER]]
        w_f32 = work[:, 0:4 * D].rearrange("p (u n) -> p u n", u=2)
        diff = work[:, 4 * D:6 * D].rearrange("p (u n) -> p u n", u=2)
        gated = work[:, 6 * D:8 * D].rearrange("p (u n) -> p u n", u=2)
        h_f32 = work[:, 8 * D:10 * D].rearrange("p (u n) -> p u n", u=2)
        probs = sb("probs", [P, 2, P], F32)
        ident = sb("ident", [P, P], F32)
        scale_flat = sb("scale_flat", [P, 2 * GI * INTER // P + GD * D // P], F32)
        lane = sb("lane", [P, 4], I32)
        pick = sb("pick", [P, 1], F32)
        half_pow = sb("half_pow", [P, 1], F32)
        gates = sb("gates", [P, 2], F32)
        tanhs = sb("tanhs", [P, 2], F32)
        top = sb("top", [P, 8], F32)
        top2 = sb("top2", [P, 16], F32)
        exp2 = top2[:, 0:3]
        inv2 = top2[:, 3:6]
        c_w = top2[:, 6:9]
        tanh_scale = top2[:, 10:11]
        tau_a = top2[:, 11:12]
        tau = top2[:, 12:13]
        stats = sb("stats", [P, 2, B, 6], F32)
        mv = sb("mv", [P, 2, B, 2], F32)
        veps = sb("veps", [P, 2, B], F32)
        rstd = sb("rstd", [P, 2, B], F32)
        shift = sb("shift", [P, 2, B], F32)
        smax = sb("smax", [P, 4, B], F32)

        psum = stack.enter_context(nc.psum_tensor("psum", [P, 8, 512], F32))
        ctxT_ps, queryT_ps, nT_ps = psum[:, 0], psum[:, 1], psum[:, 3]
        score_ps, value_ps = psum[:, 2, 0:P], psum[:, 2]
        gate_ps, up_ps, s_ps, z_ps = psum[:, 4], psum[:, 5], psum[:, 6], psum[:, 7]

        x_in = [sem(f"x_in{b}") for b in range(B)]
        ctx_loaded = [sem(f"ctx_loaded{b}") for b in range(B)]
        gates_in, flat_in, rows_in, zeros_in, idx_in, idx_down_in = (sem(n) for n in ("gates_in", "flat_in", "rows_in", "zeros_in", "idx_in", "idx_down_in"))
        qw_in, qd_in = sem("qw_in"), sem("qd_in")
        const_made, ident_made, rows_cleared = sem("const_made"), sem("ident_made"), sem("rows_cleared")
        lane_made = sem("lane_made")
        stats_made, mv_made, veps_made, rstd_made, shift_made = (sem(n) for n in ("stats_made", "mv_made", "veps_made", "rstd_made", "shift_made"))
        normed_made, query_made = sem("normed_made"), sem("query_made")
        turned, turned_copied = sem("turned"), sem("turned_copied")
        scored, max_made, bias_made, exp_made = sem("scored"), sem("max_made"), sem("bias_made"), sem("exp_made")
        inv_made, probs_made, valued, x2_made = sem("inv_made"), sem("probs_made"), sem("valued"), sem("x2_made")
        n_turned, n_hi_made, n_lo_made = sem("n_turned"), sem("n_hi_made"), sem("n_lo_made")
        part1_made, rest1_made, part2_made, part3_made = (sem(n) for n in ("part1_made", "rest1_made", "part2_made", "part3_made"))
        zeros_step, zeros_made = sem("zeros_step"), sem("zeros_made")
        idx_step, onehot_made = sem("idx_step"), sem("onehot_made")
        qw_unpacked, qd_unpacked = sem("qw_unpacked"), sem("qd_unpacked")
        own_top, all_top, scalar_step, scalars_made, tanh_made = (sem(n) for n in ("own_top", "all_top", "scalar_step", "scalars_made", "tanh_made"))
        gathered, diff_made, w_formed, w_hi_made, w_lo_made = (sem(n) for n in ("gathered", "diff_made", "w_formed", "w_hi_made", "w_lo_made"))
        gate_ready, up_ready, tanh_gate_made, gated_made, h_formed, h_hi_made, h_lo_made = (sem(n) for n in ("gate_ready", "up_ready", "tanh_gate_made", "gated_made", "h_formed", "h_hi_made", "h_lo_made"))
        down_ready, out_formed, stored = sem("down_ready"), sem("out_formed"), sem("stored")

        block = stack.enter_context(nc.Block())

        def column(vec, lo, n):
            return bass.AP(tensor=vec.tensor, offset=vec.offset + lo, ap=[[0, P], [1, n]])

        CHUNKS = [(0, 3 * P), (3 * P, 7 * P), (7 * P, NPAD), None]
        SPLIT_AT = 1

        def chunk(tile, c, lo_row=0):
            if CHUNKS[c] is None:
                return tile[lo_row:P, 2 * NPAD:TABLE]
            lo, hi = CHUNKS[c]
            return tile[lo_row:P, 0:2 * NPAD].rearrange("p (a n) -> p a n", a=2)[:, :, lo:hi]

        STEPS = B + 3
        ln_of_step = {s: [(1, s - 1)] * (1 <= s <= B) + [(0, s + 3)] * (s + 3 < B) for s in range(STEPS)}
        ln_of_step[-1] = [(0, 0), (0, 1), (0, 2)]
        ln_order = [key for s in range(-1, STEPS) for key in ln_of_step[s]]
        mv_count = {key: n + 1 for n, key in enumerate(ln_order)}

        @block.sync
        def _(sp):
            a = GI * INTER // P
            first = [(zq[0:GI, 0:INTER // 8], gate_z, zeros_in), (zq[0:GI, INTER // 8:2 * INTER // 8], up_z, zeros_in),
                     (zq[0:GD, 2 * INTER // 8:ZW], down_z, zeros_in)]
            first += [(idx_i[0][:, 0:D], column(gate_i, 0, D), idx_in), (idx_i[0][:, D:2 * D], column(up_i, 0, D), idx_in)]
            first += [(scale_flat[:, lo:hi], src.rearrange("g n -> (g n)").rearrange("(p c) -> p c", p=P), flat_in)
                      for lo, hi, src in ((0, a, gate_s), (a, 2 * a, up_s), (2 * a, 2 * a + GD * D // P, down_s))]
            first += [(gates[:, 0:1], column(g_xattn, 0, 1), gates_in), (gates[:, 1:2], column(g_ffn, 0, 1), gates_in)]
            rows = []
            for r in (0, 64, 96):
                rows += [(scale_rows[r:r + GI, 0:INTER], gate_s, rows_in), (scale_rows[r:r + GI, NPAD:NPAD + INTER], up_s, rows_in),
                         (scale_rows[r:r + GD, 2 * NPAD:TABLE], down_s, rows_in)]
            words = [(qw[64 * h:64 * h + 64, tb, 0:INTER], src, qw_in)
                     for h in range(2) for tb, src in enumerate((gate_q, up_q))]
            for b in range(B):
                sp.dma_start(x_sb[:, b, :], x[b]).then_inc(x_in[b], 16)
                sp.dma_start(ctx_sb[:, b, :], ctx_in[b]).then_inc(ctx_loaded[b], 16)
                if b == 2:
                    sp.wait_ge(rows_cleared, 3)
                for dst, src, landed in {1: first, 2: rows, 3: words}.get(b, []):
                    sp.dma_start(dst, src).then_inc(landed, 16)
            for i in range(NT):
                rows = min(P, INTER - i * P) // 8
                src = bass.AP(tensor=down_q.tensor, offset=down_q.offset + 16 * i * D, ap=[[D, rows], [0, 8], [1, D]])
                sp.dma_start(qd[0:8 * rows, i, :], src).then_inc(qd_in, 16)
            sp.wait_ge(part3_made, len(CHUNKS))
            sp.dma_start(idx_i[1], column(down_i, 0, INTER)).then_inc(idx_down_in, 16)
            with sp.Fori(0, B) as m:
                sp.wait_ge(out_formed, m + 1)
                sp.dma_start(out[bass.ds(m, 1)].rearrange("a s d -> (a s) d"), x_sb[:, bass.ds(m, 1), :].rearrange("p a d -> p (a d)")).then_inc(stored, 16)
            sp.wait_ge(stored, 16 * B)

        @block.gpsimd
        def _(pool):
            pool.memset(scale_rows, 0.0).then_inc(rows_cleared, 1)
            pool.memset(qd[:, NT - 1, :], 0).then_inc(rows_cleared, 1)
            pool.memset(table_z[:, :].bitcast(I32), 0).then_inc(const_made, 1)
            pool.memset(ident[:, :], 0.0).then_inc(ident_made, 1)
            pool.wait_ge(ident_made, 1)
            pool.affine_select(out=ident[:, :], in_=ident[:, :], compare_op=ALU.not_equal, fill=1.0, base=0,
                               pattern=[[-1, P]], channel_multiplier=1).then_inc(ident_made, 1)
            pool.memset(qw[:, :, INTER:NPAD], 0).then_inc(rows_cleared, 1)
            pool.iota(lane[:, 0:1], pattern=[[0, 1]], base=0, channel_multiplier=1).then_inc(const_made, 1)
            pool.memset(half_pow[:, :], -0.5).then_inc(const_made, 1)

            def rstds(ln, b):
                n = mv_count[ln, b]
                pool.wait_ge(mv_made, n)
                pool.tensor_scalar(veps[:, ln, b:b + 1], mv[:, ln, b, 1:2], EPS, None, ALU.add).then_inc(veps_made, 1)
                pool.wait_ge(veps_made, n)
                pool.tensor_tensor(rstd[:, ln, b:b + 1], veps[:, ln, b:b + 1], half_pow[:, :], ALU.pow).then_inc(rstd_made, 1)
                pool.wait_ge(rstd_made, n)
                pool.tensor_scalar(shift[:, ln, b:b + 1], mv[:, ln, b, 0:1], rstd[:, ln, b:b + 1], -1.0,
                                   ALU.mult, ALU.mult).then_inc(shift_made, 1)

            def rest1(c):
                pool.wait_ge(part1_made, c + 1)
                pool.tensor_tensor(chunk(scale_rows, c, 64), chunk(scale_rows, c, 64), chunk(table_s, c, 64), ALU.subtract).then_inc(rest1_made, 1)
                pool.wait_ge(rest1_made, c + 1)

            def rest2(c):
                pool.wait_ge(part2_made, c + 1)
                pool.tensor_tensor(chunk(table_s, c, 96), chunk(scale_rows, c, 96), chunk(table_s, c, 96), ALU.subtract).then_inc(part3_made, 1)
                pool.wait_ge(part3_made, c + 1)

            def low_w_gate_up(i, u):
                pool.wait_ge(w_hi_made, i + 1)
                pool.tensor_tensor(flat(w_lo[:, at(i), :, :]), w_f32[:, u, :], flat(w_hi[:, at(i), :, :]), ALU.subtract).then_inc(w_lo_made, 1)

            def low_w_down(i, u):
                pool.wait_ge(w_hi_made, NT + i + 1)
                pool.tensor_tensor(flat(wd[:, at(i), 1]), w_f32[:, u, 0:D], flat(wd[:, at(i), 0]), ALU.subtract).then_inc(w_lo_made, 1)

            def low_h(half, i, u):
                pool.wait_ge(h_hi_made, half * NT + i + 1)
                pool.tensor_tensor(flat(hidden[:, half, at(i), 1, :]), h_f32[:, u, :], flat(hidden[:, half, at(i), 0, :]),
                                   ALU.subtract).then_inc(h_lo_made, 1)

            def attention_step(s):
                for ln, b in ln_of_step[s]:
                    rstds(ln, b)
                if s == 1:
                    pool.wait_ge(own_top, 3)
                    pool.partition_all_reduce(top[:, 3:6], top[:, 0:3], P, ABSMAX).then_inc(all_top, 1)
                    pool.wait_ge(all_top, 1)
                c = s - SPLIT_AT
                if 0 <= c <= len(CHUNKS):
                    pool.wait_ge(shift_made, mv_count[ln_of_step[s][-1]])
                    if s > FIRST_MIXED - 1:
                        pool.wait_ge(w_lo_made, s - FIRST_MIXED + 3)
                    if c >= 1:
                        rest2(c - 1)
                    if c < len(CHUNKS):
                        rest1(c)

            def first_half(i, u):
                if not isinstance(i, int) or i + 2 < NT:
                    low_w_gate_up(i + 2, u)
                low_h(0, i, u)

            def second_half(i, u):
                low_w_down(i, u)
                low_h(1, i, u)

            pool.wait_ge(const_made, 3)
            for s in range(-1, FIRST_MIXED):
                attention_step(s)
            for i in range(2):
                low_w_gate_up(i, i)
            run_first(pool, first_half, attention_step)
            run_second(pool, second_half)

        @block.vector
        def _(dve):
            def ln_stats(ln, b):
                n = mv_count[ln, b]
                if ln == 0:
                    dve.wait_ge(x_in[b], 16)
                else:
                    dve.wait_ge(x2_made, b + 1)
                dve.bn_stats(stats[:, ln, b, :], x_sb[:, b, :]).then_inc(stats_made, 1)
                dve.wait_ge(stats_made, n)
                dve.bn_aggr(mv[:, ln, b, :], stats[:, ln, b, :]).then_inc(mv_made, 1)

            def score_max(b):
                dve.wait_ge(scored, b + 1)
                dve.tensor_reduce(smax[:, 0, b:b + 1], score_ps, AX_X, ALU.max, negate=True).then_inc(max_made, 1)
                dve.wait_ge(max_made, b + 1)
                dve.tensor_scalar(smax[:, 1, b:b + 1], smax[:, 0, b:b + 1], SCALE, None, ALU.mult).then_inc(bias_made, 1)

            def normalise(b):
                dve.wait_ge(exp_made, b + 1)
                dve.reciprocal(smax[:, 3, b:b + 1], smax[:, 2, b:b + 1]).then_inc(inv_made, 1)
                dve.wait_ge(inv_made, b + 1)
                dve.tensor_scalar(probs[:, b % 2, :], probs[:, b % 2, :], smax[:, 3, b:b + 1], None, ALU.mult).then_inc(probs_made, 1)

            def residual(b):
                dve.wait_ge(valued, b + 1)
                if b == 0:
                    dve.wait_ge(tanh_made, 1)
                dve.wait_ge(query_made, b + 1)
                dve.scalar_tensor_tensor(out=x_sb[:, b, :], in0=value_ps, scalar=tanhs[:, 0:1], in1=x_sb[:, b, :],
                                         op0=ALU.mult, op1=ALU.add).then_inc(x2_made, 1)

            def n_low(b):
                dve.wait_ge(n_hi_made, b + 1)
                dve.scalar_tensor_tensor(out=nT_lo[:, :, b * S:(b + 1) * S], in0=nT_ps.rearrange("p (t m) -> p t m", t=KT),
                                         scalar=2.0 ** XBITS, in1=nT_hi[:, :, b * S:(b + 1) * S],
                                         op0=ALU.mult, op1=ALU.subtract).then_inc(n_lo_made, 1)

            def lanes():
                dve.wait_ge(const_made, 3)
                dve.tensor_scalar(lane[:, 1:2], lane[:, 0:1], 31, None, ALU.bitwise_and).then_inc(lane_made, 1)
                dve.tensor_scalar(lane[:, 2:3], lane[:, 0:1], 7, 2, ALU.bitwise_and, ALU.logical_shift_left).then_inc(lane_made, 1)
                dve.memset(lane[:, 3:4], 15).then_inc(lane_made, 1)
                dve.wait_ge(lane_made, 3)
                dve.tensor_copy(pick[:, :], lane[:, 1:2]).then_inc(lane_made, 1)

            def own_tops():
                dve.wait_ge(flat_in, 48)
                a, bb = GI * INTER // P, 2 * GI * INTER // P
                for n, (lo, hi) in enumerate(((0, a), (a, bb), (bb, bb + GD * D // P))):
                    dve.tensor_reduce(top[:, n:n + 1], scale_flat[:, lo:hi], AX_X, ALU.max,
                                      apply_absolute_value=True).then_inc(own_top, 1)

            def scalars():
                dve.wait_ge(all_top, 1)
                dve.tensor_scalar(top[:, 3:6], top[:, 3:6], FLOOR, None, ALU.max).then_inc(scalar_step, 1)
                dve.wait_ge(scalar_step, 1)
                dve.tensor_scalar(exp2.bitcast(I32), top[:, 3:6].bitcast(I32), 0x7F800000, None, ALU.bitwise_and).then_inc(scalar_step, 1)
                dve.wait_ge(scalar_step, 2)
                dve.reciprocal(inv2, exp2).then_inc(scalar_step, 1)
                dve.wait_ge(scalar_step, 3)
                dve.tensor_scalar(c_w, inv2, 2.0 ** WBITS, None, ALU.mult).then_inc(scalars_made, 1)
                dve.tensor_scalar(tanh_scale, exp2[:, 0:1], 2.0 ** -(XBITS + WBITS + 1), None, ALU.mult).then_inc(scalars_made, 1)
                dve.scalar_tensor_tensor(out=tau_a, in0=exp2[:, 0:1], scalar=2.0 ** -(XBITS + 2 * WBITS + KBITS), in1=exp2[:, 1:2],
                                         op0=ALU.mult, op1=ALU.mult).then_inc(scalar_step, 1)
                dve.wait_ge(scalar_step, 4)
                dve.wait_ge(tanh_made, 1)
                dve.scalar_tensor_tensor(out=tau, in0=tau_a, scalar=exp2[:, 2:3], in1=tanhs[:, 1:2],
                                         op0=ALU.mult, op1=ALU.mult).then_inc(scalars_made, 1)

            def unpack_gate_up(part):
                lo, hi = ((0, 3 * P), (3 * P, NPAD))[part]
                dve.wait_ge(qw_in, 64)
                dve.wait_ge(rows_cleared, 3)
                dve.tensor_scalar(qw[0:64, :, lo:hi], qw[0:64, :, lo:hi], 0x0F0F0F0F, None, ALU.bitwise_and).then_inc(qw_unpacked, 1)
                dve.tensor_scalar(qw[64:P, :, lo:hi], qw[64:P, :, lo:hi], 4, 0x0F0F0F0F, ALU.logical_shift_right, ALU.bitwise_and).then_inc(qw_unpacked, 1)

            def zeros():
                dve.wait_ge(zeros_in, 48)
                zb = zq[:, :].bitcast(U8)
                two = z8[:, 0:2 * NPAD].rearrange("p (a n) -> p a n", a=2)[:, :, 0:INTER].rearrange("p a (b h) -> p a b h", h=2)
                one = z8[:, 2 * NPAD:TABLE].rearrange("p (b h) -> p b h", h=2)
                for h in range(2):
                    dve.tensor_scalar(two[0:GI, :, :, h], zb[0:GI, 0:INTER].rearrange("p (a b) -> p a b", a=2),
                                      4 * h, 15, ALU.logical_shift_right, ALU.bitwise_and).then_inc(zeros_step, 1)
                    dve.tensor_scalar(one[0:GD, :, h], zb[0:GD, INTER:INTER + D // 2],
                                      4 * h, 15, ALU.logical_shift_right, ALU.bitwise_and).then_inc(zeros_step, 1)

            def indices(part):
                groups = (GI, GD)[part]
                if part == 0:
                    dve.wait_ge(idx_in, 32)
                else:
                    dve.wait_ge(idx_down_in, 16)
                dve.tensor_scalar(idx_f[part], idx_i[part], 0.0, float(groups), ALU.is_lt, ALU.mult).then_inc(idx_step, 1)
                dve.wait_ge(idx_step, 3 * part + 1)
                dve.tensor_tensor(idx_f[part], idx_i[part], idx_f[part], ALU.add).then_inc(idx_step, 1)
                dve.wait_ge(idx_step, 3 * part + 2)
                dve.tensor_scalar(idx_f[part], idx_f[part], 0.0, float(groups - 1), ALU.max, ALU.min).then_inc(idx_step, 1)

            def onehots(part):
                dve.wait_ge(idx_step, 3 * part + 3)
                dve.wait_ge(lane_made, 4)
                if part == 0:
                    for tb in range(2):
                        dve.tensor_scalar(onehot[:, tb * D:(tb + 1) * D].rearrange("p (t h r) -> p t h r", t=KT, h=2),
                                          idx_f[0][:, tb * D:(tb + 1) * D].rearrange("p (r t h) -> p t h r", t=KT, h=2),
                                          pick[:, :], None, ALU.is_equal).then_inc(onehot_made, 1)
                else:
                    dve.memset(onehot[:, 2 * D + INTER:2 * D + NPAD], 0.0).then_inc(onehot_made, 1)
                    dve.tensor_scalar(onehot[:, 2 * D:2 * D + INTER], idx_f[1], pick[:, :], None, ALU.is_equal).then_inc(onehot_made, 1)

            def dequant_gate_up(i, u, tb):
                if isinstance(i, int) and i < 2:
                    dve.wait_ge(qw_unpacked, 2)
                    dve.wait_ge(scalars_made, 3)
                    dve.wait_ge(onehot_made, 2)
                elif isinstance(i, int) and i == 3:
                    dve.wait_ge(qw_unpacked, 4)
                n = 2 * i + tb
                dve.wait_ge(gathered, n + 1)
                wait_if(dve, w_formed, n - 1)
                dve.tensor_tensor(diff[:, tb, :].rearrange("p (t n) -> p t n", t=KT),
                                  qw[:, tb, :].bitcast(U8).rearrange("p (n t) -> p t n", t=KT)[:, :, at(i * P, P)],
                                  z_ps.rearrange("p (t n) -> p t n", t=KT), ALU.subtract).then_inc(diff_made, 1)
                dve.wait_ge(diff_made, n + 1)
                wait_if(dve, w_lo_made, i - 1)
                dve.scalar_tensor_tensor(out=w_f32[:, u, tb * D:(tb + 1) * D], in0=diff[:, tb, :], scalar=c_w[:, tb:tb + 1],
                                         in1=s_ps, op0=ALU.mult, op1=ALU.mult).then_inc(w_formed, 1)

            def dequant_down(i, u):
                dve.wait_ge(gathered, 2 * NT + i + 1)
                dve.wait_ge(w_formed, 2 * NT + i)
                dve.tensor_tensor(diff[:, 0, :], flat(qd[:, at(i), :]), z_ps, ALU.subtract).then_inc(diff_made, 1)
                dve.wait_ge(diff_made, 2 * NT + i + 1)
                dve.wait_ge(w_lo_made, NT + i - 1)
                dve.scalar_tensor_tensor(out=w_f32[:, u, 0:D], in0=diff[:, 0, :], scalar=c_w[:, 2:3], in1=s_ps,
                                         op0=ALU.mult, op1=ALU.mult).then_inc(w_formed, 1)

            def form_gated(n, u):
                dve.wait_ge(tanh_gate_made, n + 1)
                dve.scalar_tensor_tensor(out=gated[:, u, :], in0=gated[:, u, :], scalar=1.0, in1=gate_ps,
                                         op0=ALU.add, op1=ALU.mult).then_inc(gated_made, 1)

            def form_hidden(n, u):
                dve.wait_ge(up_ready, n + 1)
                dve.wait_ge(gated_made, n + 1)
                wait_if(dve, h_lo_made, n - 1)
                dve.scalar_tensor_tensor(out=h_f32[:, u, :], in0=gated[:, u, :], scalar=2.0 ** (KBITS - XBITS - WBITS - 1), in1=up_ps,
                                         op0=ALU.mult, op1=ALU.mult).then_inc(h_formed, 1)

            between = {4: [lambda: dequant_gate_up(0, 0, 0)], 5: [lambda: dequant_gate_up(1, 1, 0)]}
            after = {1: [lambda: onehots(0)], 2: [scalars, lambda: unpack_gate_up(0)],
                     4: [lambda: dequant_gate_up(0, 0, 1)], 5: [lambda: dequant_gate_up(1, 1, 1)], 6: [lambda: unpack_gate_up(1)],
                     9: [lambda: indices(1)], 10: [lambda: onehots(1)]}

            def attention_step(s):
                if 1 <= s <= B:
                    residual(s - 1)
                if s >= 3 and s != FIRST_MIXED:
                    n_low(s - 3)
                for ln, b in ln_of_step[s]:
                    if ln == 1:
                        ln_stats(ln, b)
                for piece in between.get(s, []):
                    piece()
                if s < B:
                    score_max(s)
                    normalise(s)
                for ln, b in ln_of_step[s]:
                    if ln == 0:
                        ln_stats(ln, b)
                for piece in after.get(s, []):
                    piece()

            def first_half(i, u):
                if not isinstance(i, int) or i + 2 < NT:
                    dequant_gate_up(i + 2, u, 0)
                    dequant_gate_up(i + 2, u, 1)
                if isinstance(i, int) and i == NT - 2:
                    dve.wait_ge(qd_in, 16 * NT)
                    dve.tensor_scalar(qd[:, :, :], qd[:, :, :], lane[:, 2:3], lane[:, 3:4], ALU.logical_shift_right,
                                      ALU.bitwise_and).then_inc(qd_unpacked, 1)
                form_gated(i, u)
                form_hidden(i, u)

            def second_half(i, u):
                dequant_down(i, u)
                form_gated(NT + i, u)
                form_hidden(NT + i, u)

            ln_stats(0, 0)
            ln_stats(0, 1)
            lanes()
            zeros()
            indices(0)
            own_tops()
            ln_stats(0, 2)
            for s in range(FIRST_MIXED):
                attention_step(s)
            n_low(FIRST_MIXED - 3)
            run_first(dve, first_half, attention_step)
            dve.wait_ge(qd_unpacked, 1)
            run_second(dve, second_half)

            with dve.Fori(0, B) as m:
                dve.wait_ge(down_ready, m + 1)
                row = flat(x_sb[:, at(m), :])
                dve.scalar_tensor_tensor(out=row, in0=flat(psum[:, at(m), :]), scalar=tau, in1=row,
                                         op0=ALU.mult, op1=ALU.add).then_inc(out_formed, 1)

        @block.scalar
        def _(act):
            def copies(b):
                act.wait_ge(turned, b + 1)
                if b >= 2:
                    act.wait_ge(scored, b - 1)
                act.activation(ctxT[:, b % 2, :], ctxT_ps, ACT.Copy).then_inc(turned_copied, 1)
                act.activation(queryT[:, b % 2, :], queryT_ps, ACT.Copy).then_inc(turned_copied, 1)

            def make_query(b):
                act.wait_ge(shift_made, mv_count[0, b])
                if b >= 2:
                    act.wait_ge(turned, b - 1)
                act.activation(query[:, b % 2, :], x_sb[:, b, :], ACT.Identity, bias=shift[:, 0, b:b + 1],
                               scale=rstd[:, 0, b:b + 1]).then_inc(query_made, 1)

            def make_normed(b):
                act.wait_ge(shift_made, mv_count[1, b])
                if b >= 2:
                    act.wait_ge(n_turned, b - 1)
                act.activation(normed[:, b % 2, :].rearrange("p (t h r) -> p t h r", t=KT, h=2),
                               x_sb[:, b, :].rearrange("p (r t h) -> p t h r", t=KT, h=2), ACT.Identity,
                               bias=shift[:, 1, b:b + 1], scale=rstd[:, 1, b:b + 1]).then_inc(normed_made, 1)

            def part1(c):
                act.wait_ge(rows_in, 16 * 9)
                act.activation(chunk(table_s, c), chunk(scale_rows, c), ACT.Copy).then_inc(part1_made, 1)

            def part2(c):
                act.wait_ge(rest1_made, c + 1)
                act.activation(chunk(table_s, c, 64), chunk(scale_rows, c, 64), ACT.Copy).then_inc(part2_made, 1)

            def zero_rows(n):
                lo, hi, g = ((0, INTER, GI), (NPAD, NPAD + INTER, GI), (2 * NPAD, TABLE, GD))[n]
                act.wait_ge(zeros_step, 4)
                act.activation(table_z[0:g, lo:hi], z8[0:g, lo:hi], ACT.Copy, bias=1.0).then_inc(zeros_made, 1)

            def exponentials(b):
                act.wait_ge(bias_made, b + 1)
                if b >= 2:
                    act.wait_ge(valued, b - 1)
                act.activation(probs[:, b % 2, :], score_ps, ACT.Exp, bias=smax[:, 1, b:b + 1], scale=SCALE,
                               accum_out=smax[:, 2, b:b + 1]).then_inc(exp_made, 1)

            def n_high(b):
                act.wait_ge(n_turned, b + 1)
                act.activation(nT_hi[:, :, b * S:(b + 1) * S], nT_ps.rearrange("p (t m) -> p t m", t=KT),
                               ACT.Copy, scale=2.0 ** XBITS).then_inc(n_hi_made, 1)

            def high_w_gate_up(i, u):
                act.wait_ge(w_formed, 2 * i + 2)
                act.activation(flat(w_hi[:, at(i), :, :]), w_f32[:, u, :], ACT.Copy).then_inc(w_hi_made, 1)

            def high_w_down(i, u):
                act.wait_ge(w_formed, 2 * NT + i + 1)
                act.activation(flat(wd[:, at(i), 0]), w_f32[:, u, 0:D], ACT.Copy).then_inc(w_hi_made, 1)

            def gate_tanh(n, u):
                act.wait_ge(gate_ready, n + 1)
                wait_if(act, h_formed, n - 1)
                act.activation(gated[:, u, :], gate_ps, ACT.Tanh, scale=tanh_scale).then_inc(tanh_gate_made, 1)

            def high_h(half, i, u):
                act.wait_ge(h_formed, half * NT + i + 1)
                act.activation(flat(hidden[:, half, at(i), 0, :]), h_f32[:, u, :], ACT.Copy).then_inc(h_hi_made, 1)

            def attention_step(s):
                if s >= 3 and s != FIRST_MIXED:
                    n_high(s - 3)
                if 2 <= s < B + 2:
                    make_normed(s - 2)
                if s + 1 < B:
                    copies(s + 1)
                if s + 2 < B:
                    make_query(s + 2)
                if s < B:
                    exponentials(s)
                if s == 5:
                    high_w_gate_up(0, 0)
                if 0 < s - SPLIT_AT <= len(CHUNKS):
                    part2(s - SPLIT_AT - 1)
                if 0 <= s - SPLIT_AT < len(CHUNKS):
                    part1(s - SPLIT_AT)
                if s < 3:
                    zero_rows(s)

            def first_half(i, u):
                gate_tanh(i, u)
                if not isinstance(i, int) or i + 2 < NT:
                    high_w_gate_up(i + 2, u)
                high_h(0, i, u)

            def second_half(i, u):
                high_w_down(i, u)
                gate_tanh(NT + i, u)
                high_h(1, i, u)

            make_query(0)
            make_query(1)
            copies(0)
            act.wait_ge(gates_in, 32)
            act.activation(tanhs[:, :], gates[:, :], ACT.Tanh).then_inc(tanh_made, 1)
            for s in range(FIRST_MIXED):
                attention_step(s)
            n_high(FIRST_MIXED - 3)
            high_w_gate_up(1, 1)
            run_first(act, first_half, attention_step)
            run_second(act, second_half)

        @block.tensor
        def _(pe):
            def turn(b):
                pe.wait_ge(ctx_loaded[b], 16)
                if b >= 1:
                    pe.wait_ge(turned_copied, 2 * b)
                for t in range(KT):
                    pe.transpose(ctxT_ps[:, t * P:(t + 1) * P], ctx_sb[:, b, t * P:(t + 1) * P], ident[:, :])
                pe.wait_ge(query_made, b + 1)
                for t in range(KT):
                    mm = pe.transpose(queryT_ps[:, t * P:(t + 1) * P], query[:, b % 2, t * P:(t + 1) * P], ident[:, :])
                mm.then_inc(turned, 1)

            def scores(b):
                pe.wait_ge(turned_copied, 2 * (b + 1))
                if b:
                    pe.wait_ge(x2_made, b)
                for t in range(KT):
                    mm = pe.matmul(score_ps, queryT[:, b % 2, t * P:(t + 1) * P], ctxT[:, b % 2, t * P:(t + 1) * P],
                                   start=(t == 0), stop=(t == KT - 1))
                mm.then_inc(scored, 1)

            def values(b):
                pe.wait_ge(probs_made, b + 1)
                pe.matmul(value_ps, probs[:, b % 2, :], ctx_sb[:, b, :], start=True, stop=True).then_inc(valued, 1)

            def turn_normed(b):
                pe.wait_ge(normed_made, b + 1)
                if b >= 1:
                    pe.wait_ge(n_lo_made, b)
                for t in range(KT):
                    mm = pe.transpose(nT_ps[:, t * P:(t + 1) * P], normed[:, b % 2, t * P:(t + 1) * P], ident[:, :])
                mm.then_inc(n_turned, 1)

            def gather_gate_up(i, tb):
                if isinstance(i, int) and tb == 0:
                    pe.wait_ge(part3_made, 1 if i < 3 else 2 if i < 6 else 3)
                    if i == 0:
                        pe.wait_ge(zeros_made, 3)
                        pe.wait_ge(onehot_made, 2)
                wait_if(pe, w_formed, 2 * i + tb)
                scale_cols = table_s[:, at(i * P + tb * NPAD, P)]
                zero_cols = table_z[:, at(i * P + tb * NPAD, P)]
                for t in range(KT):
                    k = slice(tb * D + t * P, tb * D + (t + 1) * P)
                    pe.matmul(s_ps[:, t * P:(t + 1) * P], onehot[:, k], scale_cols, start=True, stop=True)
                    mm = pe.matmul(z_ps[:, t * P:(t + 1) * P], onehot[0:32, k], zero_cols, start=True, stop=True)
                mm.then_inc(gathered, 1)

            def gather_down(i):
                pe.wait_ge(w_formed, 2 * NT + i)
                k = at(i * P + 2 * D, P)
                pe.matmul(s_ps, onehot[:, k], table_s[:, 2 * NPAD:TABLE], start=True, stop=True)
                pe.matmul(z_ps, onehot[0:32, k], table_z[:, 2 * NPAD:TABLE], start=True, stop=True).then_inc(gathered, 1)

            def project(half, i, tb):
                n = half * NT + i
                if tb == 0:
                    if half == 0:
                        pe.wait_ge(w_lo_made, i + 1)
                    wait_if(pe, gated_made, n)
                else:
                    wait_if(pe, h_formed, n)
                acc, tok = (gate_ps, up_ps)[tb], slice(half * HALF, (half + 1) * HALF)
                for t in range(KT):
                    hi = flat(w_hi[:, at(i), tb, t * P:(t + 1) * P])
                    lo = flat(w_lo[:, at(i), tb, t * P:(t + 1) * P])
                    pe.matmul(acc, hi, nT_hi[:, t, tok], start=(t == 0), stop=False)
                    pe.matmul(acc, hi, nT_lo[:, t, tok], start=False, stop=False)
                    mm = pe.matmul(acc, lo, nT_hi[:, t, tok], start=False, stop=(t == KT - 1))
                mm.then_inc((gate_ready, up_ready)[tb], 1)

            def attention_step(s):
                if s in (4, 5):
                    gather_gate_up(s - 4, 0)
                if 1 <= s <= B:
                    values(s - 1)
                if s + 1 < B:
                    turn(s + 1)
                if s < B:
                    scores(s)
                if 2 <= s < B + 2:
                    turn_normed(s - 2)
                if s in (4, 5):
                    gather_gate_up(s - 4, 1)

            def first_half(i, u):
                for tb in range(2):
                    if not isinstance(i, int) or i + 2 < NT:
                        gather_gate_up(i + 2, tb)
                    if isinstance(i, int) and i + tb == 0:
                        pe.wait_ge(n_lo_made, BH)
                    project(0, i, tb)

            def second_half(i, u):
                gather_down(i)
                project(1, i, 0)
                project(1, i, 1)

            pe.wait_ge(ident_made, 2)
            turn(0)
            for s in range(FIRST_MIXED):
                attention_step(s)
            run_first(pe, first_half, attention_step)
            pe.wait_ge(part3_made, len(CHUNKS))
            pe.wait_ge(onehot_made, 4)
            pe.wait_ge(n_lo_made, B)
            run_second(pe, second_half)

            pe.wait_ge(w_lo_made, 2 * NT)
            for half in range(2):
                pe.wait_ge(h_lo_made, (half + 1) * NT)
                with pe.Fori(0, BH) as m:
                    acc = flat(psum[:, at(m + half * BH), :])
                    for i in range(NT):
                        hi = flat(hidden[:, half, i:i + 1, 0, at(m * P, P)])
                        lo = flat(hidden[:, half, i:i + 1, 1, at(m * P, P)])
                        pe.matmul(acc, hi, wd[:, i, 0], start=(i == 0), stop=False)
                        pe.matmul(acc, hi, wd[:, i, 1], start=False, stop=False)
                        mm = pe.matmul(acc, lo, wd[:, i, 0], start=False, stop=(i == NT - 1))
                    mm.then_inc(down_ready, 1)


_INS = ["x", "ctx_4096", "g_xattn", "g_ffn"] + [f"L0_ffn_{m}_{part}" for m in ("gate", "up", "down")
                                                 for part in ("qweight", "scales", "qzeros", "g_idx")]
_OUTS = [((8, 128, 512), "float32")]


def kernel(**inputs):
    import numpy as _np
    import concourse.bacc as _bacc
    from concourse import mybir as _mybir
    from concourse.bass_utils import run_bass_kernel_spmd as _run

    nc = _bacc.Bacc("TRN2", target_bir_lowering=False, num_devices=1)
    arrays, args = {}, []
    for name in _INS:
        a = _np.ascontiguousarray(inputs[name])
        arrays[f"in_{name}_dram"] = a
        args.append(nc.dram_tensor(f"in_{name}_dram", a.shape, _mybir.dt.from_np(a.dtype), kind="ExternalInput").ap())
    for n, (shape, dtype) in enumerate(_OUTS):
        dt = _mybir.dt.from_np(_np.dtype(dtype))
        args.append(nc.dram_tensor(f"out_{n}_dram", shape, dt, kind="ExternalOutput").ap())
    flamingo_gated_block(nc, *args)
    r = _run(nc, [arrays], core_ids=[0])
    return r.results[0]["out_0_dram"]
```

```python
from contextlib import ExitStack

import concourse.bass as bass
from concourse import mybir
from concourse.alu_op_type import AluOpType as ALU

ACT = mybir.ActivationFunctionType
F32 = mybir.dt.float32
F16 = mybir.dt.float16
BF16 = mybir.dt.bfloat16
I32 = mybir.dt.int32
U8 = mybir.dt.uint8
AX_X = mybir.AxisListType.X
ABSMAX = bass.bass_isa.ReduceOp.absmax

P = 128
XBITS = 10
WBITS = 10
KBITS = -33
FLOOR = 2.0 ** -30
EPS = 1e-5
PURE = 6


def at(start, size=1):
    return bass.ds(start, size)


def flat(ap):
    names = [f"d{n}" for n in range(len(ap.shape) - 1)]
    return ap.rearrange(f"p {' '.join(names)} -> p ({' '.join(names)})") if len(names) > 1 else ap


def wait_if(eng, semaphore, value):
    if not isinstance(value, int) or value > 0:
        eng.wait_ge(semaphore, value)


def run_first(eng, mixed_tile, tile):
    for i in range(4):
        mixed_tile(i, i % 2, PURE + i)
    tile(4, 0)
    with eng.Fori(0, 2) as j:
        for u in range(2):
            tile(2 * j + u + 5, 1 - u)
    for i in range(9, 11):
        tile(i, i % 2)


def run_second(eng, tile):
    with eng.Fori(0, 5) as j:
        for u in range(2):
            tile(2 * j + u, 1 - u)
    tile(10, 1)


def flamingo_gated_block(nc, x, ctx_in, g_xattn, g_ffn, gate_q, gate_s, gate_z, gate_i,
                         up_q, up_s, up_z, up_i, down_q, down_s, down_z, down_i, out):
    B, S, D = x.shape
    INTER = gate_q.shape[1]
    GI, GD = gate_s.shape[0], down_s.shape[0]
    KT = D // P
    NT = -(-INTER // P)
    NPAD = NT * P
    HALF = B * S // 2
    BH = HALF // S
    LASTK = INTER - (NT - 1) * P
    TABLE = 2 * NPAD + D
    SCALE = float(S) ** -0.5
    assert S == P and D == 512 and HALF == 512 and KT == 4 and NT == 11 and GD <= 32

    with ExitStack() as stack:
        def sb(name, shape, dt):
            return stack.enter_context(nc.sbuf_tensor(name, shape, dt))

        def sem(name):
            return stack.enter_context(nc.semaphore(name))

        EARLY = B * D + 4 * 2 * D
        shared = sb("shared", [P, EARLY + TABLE], F32)
        ctx_sb = shared[:, 0:B * D].rearrange("p (b d) -> p b d", b=B)
        early = [shared[:, (B + 2 * n) * D:(B + 2 * n + 2) * D].rearrange("p (u d) -> p u d", u=2) for n in range(4)]
        query, ctxT, queryT, normed = early
        scale_rows = shared[:, EARLY:EARLY + TABLE]
        hidden = shared[:, 0:NT * B * S].bitcast(F16).rearrange("p (h i a m) -> p h i a m", h=2, i=NT, a=2)

        x_sb = sb("x_sb", [P, B, D], F32)
        nT_hi = sb("nT_hi", [P, KT, B * S], F16)
        nT_lo = sb("nT_lo", [P, KT, B * S], F16)
        qw = sb("qw", [P, 2, NPAD], I32)
        qd = sb("qd", [P, NT, D], I32)
        wd = qd[:, :, :].bitcast(F16).rearrange("p i (a n) -> p i a n", a=2)
        w_hi = sb("w_hi", [P, NT, 2, KT * P], F16)
        w_lo = sb("w_lo", [P, NT, 2, KT * P], F16)
        table_s = sb("table_s", [P, TABLE], BF16)
        table_z = sb("table_z", [32, TABLE], BF16)
        ZW = (2 * INTER + D) // 8
        zq = sb("zq", [P, ZW], I32)
        z8 = sb("z8", [P, TABLE], U8)
        onehot = sb("onehot", [P, 2 * D + NPAD], BF16)
        work = sb("work", [P, 10 * D], F32)
        idx_i = [work[:, 0:2 * D].bitcast(I32), scale_rows[:, 0:INTER].bitcast(I32)]
        idx_f = [work[:, 2 * D:4 * D], scale_rows[:, INTER:2 * INTER]]
        w_f32 = work[:, 0:4 * D].rearrange("p (u n) -> p u n", u=2)
        diff = work[:, 4 * D:6 * D].rearrange("p (u n) -> p u n", u=2)
        gated = work[:, 6 * D:8 * D].rearrange("p (u n) -> p u n", u=2)
        h_f32 = work[:, 8 * D:10 * D].rearrange("p (u n) -> p u n", u=2)
        probs = sb("probs", [P, 2, P], F32)
        ident = sb("ident", [P, P], F32)
        scale_flat = sb("scale_flat", [P, 2 * GI * INTER // P + GD * D // P], F32)
        lane = sb("lane", [P, 4], I32)
        pick = sb("pick", [P, 1], F32)
        half_pow = sb("half_pow", [P, 1], F32)
        gates = sb("gates", [P, 2], F32)
        tanhs = sb("tanhs", [P, 2], F32)
        top = sb("top", [P, 8], F32)
        powers = sb("powers", [P, 16], F32)
        exp2 = powers[:, 0:3]
        inv2 = powers[:, 3:6]
        c_w = powers[:, 6:9]
        tanh_scale = powers[:, 10:11]
        tau_a = powers[:, 11:12]
        tau = powers[:, 12:13]
        stats = sb("stats", [P, 2, B, 6], F32)
        mv = sb("mv", [P, 2, B, 2], F32)
        veps = sb("veps", [P, 2, B], F32)
        rstd = sb("rstd", [P, 2, B], F32)
        shift = sb("shift", [P, 2, B], F32)
        smax = sb("smax", [P, 3, B], F32)

        psum = stack.enter_context(nc.psum_tensor("psum", [P, 8, 512], F32))
        ctxT_ps, queryT_ps, nT_ps = psum[:, 0], psum[:, 1], psum[:, 3]
        value_ps = psum[:, 2]
        gate_ps, up_ps, s_ps, z_ps = psum[:, 4], psum[:, 5], psum[:, 6], psum[:, 7]

        def score_bank(b):
            return (gate_ps if b < PURE else value_ps)[:, 0:P]

        x_in = [sem(f"x_in{b}") for b in range(B)]
        ctx_loaded = [sem(f"ctx_loaded{b}") for b in range(B)]
        gates_in, flat_in, rows_in, rows_down_in, zeros_in, idx_in, idx_down_in = (sem(n) for n in ("gates_in", "flat_in", "rows_in", "rows_down_in", "zeros_in", "idx_in", "idx_down_in"))
        qw_in, qd_in = sem("qw_in"), sem("qd_in")
        const_made, ident_made, rows_cleared = sem("const_made"), sem("ident_made"), sem("rows_cleared")
        lane_made = sem("lane_made")
        stats_made, mv_made, veps_made, rstd_made, shift_made = (sem(n) for n in ("stats_made", "mv_made", "veps_made", "rstd_made", "shift_made"))
        normed_made, query_made = sem("normed_made"), sem("query_made")
        turned, turned_copied = sem("turned"), sem("turned_copied")
        scored, max_made, exp_made = sem("scored"), sem("max_made"), sem("exp_made")
        inv_made, probs_made, valued, x2_made = sem("inv_made"), sem("probs_made"), sem("valued"), sem("x2_made")
        n_turned, n_hi_made, n_lo_made = sem("n_turned"), sem("n_hi_made"), sem("n_lo_made")
        part1_made, rest1_made, part2_made, part3_made = (sem(n) for n in ("part1_made", "rest1_made", "part2_made", "part3_made"))
        zeros_step, zeros_made = sem("zeros_step"), sem("zeros_made")
        idx_step, onehot_made = sem("idx_step"), sem("onehot_made")
        qw_unpacked, qd_unpacked = sem("qw_unpacked"), sem("qd_unpacked")
        own_top, all_top, scalar_step, scalars_made, tanh_made = (sem(n) for n in ("own_top", "all_top", "scalar_step", "scalars_made", "tanh_made"))
        gathered, diff_made, w_formed, w_hi_made, w_lo_made = (sem(n) for n in ("gathered", "diff_made", "w_formed", "w_hi_made", "w_lo_made"))
        gate_ready, up_ready, tanh_gate_made, gated_made, h_formed, h_hi_made, h_lo_made = (sem(n) for n in ("gate_ready", "up_ready", "tanh_gate_made", "gated_made", "h_formed", "h_hi_made", "h_lo_made"))
        down_ready, out_formed, stored = sem("down_ready"), sem("out_formed"), sem("stored")

        block = stack.enter_context(nc.Block())

        def column(vec, lo, n):
            return bass.AP(tensor=vec.tensor, offset=vec.offset + lo, ap=[[0, P], [1, n]])

        CHUNKS = [(0, 2 * P), (2 * P, 4 * P), (4 * P, 6 * P), (6 * P, 8 * P), (8 * P, NPAD), None]
        SPLIT_STEP = [0, 2, 6, 7, 8, 9]

        def chunks_for(i):
            return i // 2 + 1 if i < 6 else len(CHUNKS) - 1

        def chunk(tile, c, lo_row=0):
            if CHUNKS[c] is None:
                return tile[lo_row:P, 2 * NPAD:TABLE]
            lo, hi = CHUNKS[c]
            return tile[lo_row:P, 0:2 * NPAD].rearrange("p (a n) -> p a n", a=2)[:, :, lo:hi]

        STEPS = B + 2
        assert PURE + 4 == STEPS
        ln_of_step = {s: [(1, s - 1)] * (1 <= s <= B) + [(0, s + 3)] * (s + 3 < B) for s in range(STEPS)}
        ln_of_step[-1] = [(0, 0), (0, 1)]
        ln_of_step[0], ln_of_step[1] = [(0, 2)], [(0, 3), (1, 0), (0, 4)]
        ln_order = [key for s in range(-1, STEPS) for key in ln_of_step[s]]
        mv_count = {key: n + 1 for n, key in enumerate(ln_order)}

        @block.sync
        def _(sp):
            a = GI * INTER // P
            small = [(zq[0:GI, 0:INTER // 8], gate_z, zeros_in), (zq[0:GI, INTER // 8:2 * INTER // 8], up_z, zeros_in),
                     (zq[0:GD, 2 * INTER // 8:ZW], down_z, zeros_in)]
            small += [(idx_i[0][:, 0:D], column(gate_i, 0, D), idx_in), (idx_i[0][:, D:2 * D], column(up_i, 0, D), idx_in)]
            small += [(scale_flat[:, lo:hi], src.rearrange("g n -> (g n)").rearrange("(p c) -> p c", p=P), flat_in)
                      for lo, hi, src in ((0, a, gate_s), (a, 2 * a, up_s), (2 * a, 2 * a + GD * D // P, down_s))]
            small += [(gates[:, 0:1], column(g_xattn, 0, 1), gates_in), (gates[:, 1:2], column(g_ffn, 0, 1), gates_in)]
            rows = [(scale_rows[r:r + GI, lo:lo + INTER], src, rows_in) for r in (0, 64, 96) for lo, src in ((0, gate_s), (NPAD, up_s))]
            rows_down = [(scale_rows[r:r + GD, 2 * NPAD:TABLE], down_s, rows_down_in) for r in (0, 64, 96)]
            words = [(qw[64 * h:64 * h + 64, tb, 0:INTER], src, qw_in)
                     for h in range(2) for tb, src in enumerate((gate_q, up_q))]
            for b in range(B):
                sp.dma_start(x_sb[:, b, :], x[b]).then_inc(x_in[b], 16)
                sp.dma_start(ctx_sb[:, b, :], ctx_in[b]).then_inc(ctx_loaded[b], 16)
                for dst, src, landed in {1: small, 2: rows, 4: words, 5: rows_down}.get(b, []):
                    if landed is rows_in:
                        sp.wait_ge(rows_cleared, 1)
                    sp.dma_start(dst, src).then_inc(landed, 16)
            sp.wait_ge(rows_cleared, 2)
            for i in range(NT):
                rows = min(P, INTER - i * P) // 8
                src = bass.AP(tensor=down_q.tensor, offset=down_q.offset + 16 * i * D, ap=[[D, rows], [0, 8], [1, D]])
                sp.dma_start(qd[0:8 * rows, i, :], src).then_inc(qd_in, 16)
            sp.wait_ge(part3_made, len(CHUNKS))
            sp.dma_start(idx_i[1], column(down_i, 0, INTER)).then_inc(idx_down_in, 16)
            with sp.Fori(0, B) as m:
                sp.wait_ge(out_formed, m + 1)
                sp.dma_start(out[bass.ds(m, 1)].rearrange("a s d -> (a s) d"), x_sb[:, bass.ds(m, 1), :].rearrange("p a d -> p (a d)")).then_inc(stored, 16)
            sp.wait_ge(stored, 16 * B)

        @block.gpsimd
        def _(pool):
            pool.memset(ident[:, :], 0.0).then_inc(ident_made, 1)
            pool.wait_ge(ident_made, 1)
            pool.affine_select(out=ident[:, :], in_=ident[:, :], compare_op=ALU.not_equal, fill=1.0, base=0,
                               pattern=[[-1, P]], channel_multiplier=1).then_inc(ident_made, 1)
            pool.memset(half_pow[:, :], -0.5).then_inc(const_made, 1)
            pool.iota(lane[:, 0:1], pattern=[[0, 1]], base=0, channel_multiplier=1).then_inc(const_made, 1)
            pool.memset(scale_rows, 0.0).then_inc(rows_cleared, 1)

            def rstds(ln, b):
                n = mv_count[ln, b]
                pool.wait_ge(mv_made, n)
                pool.tensor_scalar(veps[:, ln, b:b + 1], mv[:, ln, b, 1:2], EPS, None, ALU.add).then_inc(veps_made, 1)
                pool.wait_ge(veps_made, n)
                pool.tensor_tensor(rstd[:, ln, b:b + 1], veps[:, ln, b:b + 1], half_pow[:, :], ALU.pow).then_inc(rstd_made, 1)
                pool.wait_ge(rstd_made, n)
                pool.tensor_scalar(shift[:, ln, b:b + 1], mv[:, ln, b, 0:1], rstd[:, ln, b:b + 1], -1.0,
                                   ALU.mult, ALU.mult).then_inc(shift_made, 1)

            def rest1(c):
                pool.wait_ge(part1_made, c + 1)
                pool.tensor_tensor(chunk(scale_rows, c, 64), chunk(scale_rows, c, 64), chunk(table_s, c, 64), ALU.subtract).then_inc(rest1_made, 1)
                pool.wait_ge(rest1_made, c + 1)

            def rest2(c):
                pool.wait_ge(part2_made, c + 1)
                pool.tensor_tensor(chunk(table_s, c, 96), chunk(scale_rows, c, 96), chunk(table_s, c, 96), ALU.subtract).then_inc(part3_made, 1)
                pool.wait_ge(part3_made, c + 1)

            def low_w_gate_up(i, u):
                pool.wait_ge(w_hi_made, i + 1)
                pool.tensor_tensor(flat(w_lo[:, at(i), :, :]), w_f32[:, u, :], flat(w_hi[:, at(i), :, :]), ALU.subtract).then_inc(w_lo_made, 1)

            def low_w_down(i, u):
                pool.wait_ge(w_hi_made, NT + i + 1)
                pool.tensor_tensor(flat(wd[:, at(i), 1]), w_f32[:, u, 0:D], flat(wd[:, at(i), 0]), ALU.subtract).then_inc(w_lo_made, 1)

            def low_h(half, i, u):
                pool.wait_ge(h_hi_made, half * NT + i + 1)
                pool.tensor_tensor(flat(hidden[:, half, at(i), 1, :]), h_f32[:, u, :], flat(hidden[:, half, at(i), 0, :]),
                                   ALU.subtract).then_inc(h_lo_made, 1)

            def split_table(s):
                for c in range(len(CHUNKS)):
                    if s == SPLIT_STEP[c] + 1:
                        rest2(c)
                    if s == SPLIT_STEP[c]:
                        rest1(c)

            def attention_step(s):
                for ln, b in ln_of_step[s][:2]:
                    rstds(ln, b)
                if s < 2:
                    pool.wait_ge(rows_cleared, 3)
                    pool.wait_ge(shift_made, mv_count[ln_of_step[s][:2][-1]])
                    split_table(s)
                for ln, b in ln_of_step[s][2:]:
                    rstds(ln, b)
                if s == 0:
                    pool.wait_ge(own_top, 3)
                    pool.partition_all_reduce(top[:, 3:6], top[:, 0:3], P, ABSMAX).then_inc(all_top, 1)
                    pool.wait_ge(all_top, 1)
                if s == 4:
                    low_w_gate_up(0, 0)
                if s >= 2:
                    pool.wait_ge(shift_made, mv_count[ln_of_step[s][-1]])
                    split_table(s)

            def mixed_tile(i, u, s):
                for ln, b in ln_of_step[s]:
                    rstds(ln, b)
                    pool.wait_ge(shift_made, mv_count[ln, b])
                if i >= 1:
                    pool.wait_ge(h_lo_made, i)
                split_table(s)
                if i == 0:
                    low_w_gate_up(1, 1)
                low_w_gate_up(i + 2, u)
                low_h(0, i, u)

            def first_half(i, u):
                if isinstance(i, int) and i == 4:
                    pool.wait_ge(h_lo_made, i)
                    split_table(STEPS)
                if not isinstance(i, int) or i + 2 < NT:
                    low_w_gate_up(i + 2, u)
                low_h(0, i, u)

            def second_half(i, u):
                low_w_down(i, u)
                low_h(1, i, u)

            pool.wait_ge(const_made, 3)
            for ln, b in ln_of_step[-1]:
                rstds(ln, b)
            pool.memset(qd[:, NT - 1, :], 0).then_inc(rows_cleared, 1)
            pool.memset(qw[:, :, INTER:NPAD], 0).then_inc(rows_cleared, 1)
            for s in range(PURE):
                attention_step(s)
            run_first(pool, mixed_tile, first_half)
            run_second(pool, second_half)

        @block.vector
        def _(dve):
            def ln_sums(ln, b):
                if ln == 0:
                    dve.wait_ge(x_in[b], 16)
                else:
                    dve.wait_ge(x2_made, b + 1)
                dve.bn_stats(stats[:, ln, b, :], x_sb[:, b, :]).then_inc(stats_made, 1)

            def ln_moments(ln, b):
                dve.wait_ge(stats_made, mv_count[ln, b])
                dve.bn_aggr(mv[:, ln, b, :], stats[:, ln, b, :]).then_inc(mv_made, 1)

            def score_max(b):
                dve.wait_ge(scored, b + 1)
                dve.tensor_reduce(smax[:, 0, b:b + 1], score_bank(b), AX_X, ALU.max, negate=True).then_inc(max_made, 1)

            def invert_sum(b):
                dve.wait_ge(exp_made, b + 1)
                dve.reciprocal(smax[:, 2, b:b + 1], smax[:, 1, b:b + 1]).then_inc(inv_made, 1)

            def normalise(b):
                dve.wait_ge(inv_made, b + 1)
                dve.tensor_scalar(probs[:, b % 2, :], probs[:, b % 2, :], smax[:, 2, b:b + 1], None, ALU.mult).then_inc(probs_made, 1)

            def residual(b):
                dve.wait_ge(valued, b + 1)
                if b == 0:
                    dve.wait_ge(tanh_made, 1)
                dve.wait_ge(query_made, b + 1)
                dve.scalar_tensor_tensor(out=x_sb[:, b, :], in0=value_ps, scalar=tanhs[:, 0:1], in1=x_sb[:, b, :],
                                         op0=ALU.mult, op1=ALU.add).then_inc(x2_made, 1)

            def n_low(b):
                dve.wait_ge(n_hi_made, b + 1)
                dve.scalar_tensor_tensor(out=nT_lo[:, :, b * S:(b + 1) * S], in0=nT_ps.rearrange("p (t m) -> p t m", t=KT),
                                         scalar=2.0 ** XBITS, in1=nT_hi[:, :, b * S:(b + 1) * S],
                                         op0=ALU.mult, op1=ALU.subtract).then_inc(n_lo_made, 1)

            def lanes():
                dve.wait_ge(const_made, 3)
                dve.tensor_scalar(lane[:, 1:2], lane[:, 0:1], 31, None, ALU.bitwise_and).then_inc(lane_made, 1)
                dve.tensor_scalar(lane[:, 2:3], lane[:, 0:1], 7, 2, ALU.bitwise_and, ALU.logical_shift_left).then_inc(lane_made, 1)
                dve.memset(lane[:, 3:4], 15).then_inc(lane_made, 1)
                dve.wait_ge(lane_made, 3)
                dve.tensor_copy(pick[:, :], lane[:, 1:2]).then_inc(lane_made, 1)

            def own_tops():
                dve.wait_ge(flat_in, 48)
                a, bb = GI * INTER // P, 2 * GI * INTER // P
                for n, (lo, hi) in enumerate(((0, a), (a, bb), (bb, bb + GD * D // P))):
                    dve.tensor_reduce(top[:, n:n + 1], scale_flat[:, lo:hi], AX_X, ALU.max,
                                      apply_absolute_value=True).then_inc(own_top, 1)

            def scalars(n):
                if n == 0:
                    dve.wait_ge(all_top, 1)
                    dve.tensor_scalar(top[:, 3:6], top[:, 3:6], FLOOR, None, ALU.max).then_inc(scalar_step, 1)
                elif n == 1:
                    dve.wait_ge(scalar_step, 1)
                    dve.tensor_scalar(exp2.bitcast(I32), top[:, 3:6].bitcast(I32), 0x7F800000, None, ALU.bitwise_and).then_inc(scalar_step, 1)
                elif n == 2:
                    dve.wait_ge(scalar_step, 2)
                    dve.reciprocal(inv2, exp2).then_inc(scalar_step, 1)
                    dve.scalar_tensor_tensor(out=tau_a, in0=exp2[:, 0:1], scalar=2.0 ** -(XBITS + 2 * WBITS + KBITS), in1=exp2[:, 1:2],
                                             op0=ALU.mult, op1=ALU.mult).then_inc(scalar_step, 1)
                else:
                    dve.wait_ge(scalar_step, 4)
                    dve.wait_ge(tanh_made, 1)
                    dve.tensor_scalar(c_w, inv2, 2.0 ** WBITS, None, ALU.mult).then_inc(scalars_made, 1)
                    dve.tensor_scalar(tanh_scale, exp2[:, 0:1], 2.0 ** -(XBITS + WBITS + 1), None, ALU.mult).then_inc(scalars_made, 1)
                    dve.scalar_tensor_tensor(out=tau, in0=tau_a, scalar=exp2[:, 2:3], in1=tanhs[:, 1:2],
                                             op0=ALU.mult, op1=ALU.mult).then_inc(scalars_made, 1)

            def unpack_gate_up(part):
                lo, hi = CHUNKS[part]
                dve.wait_ge(qw_in, 64)
                dve.wait_ge(rows_cleared, 3)
                dve.tensor_scalar(qw[0:64, :, lo:hi], qw[0:64, :, lo:hi], 0x0F0F0F0F, None, ALU.bitwise_and).then_inc(qw_unpacked, 1)
                dve.tensor_scalar(qw[64:P, :, lo:hi], qw[64:P, :, lo:hi], 4, 0x0F0F0F0F, ALU.logical_shift_right, ALU.bitwise_and).then_inc(qw_unpacked, 1)

            def unpack_down(i):
                if isinstance(i, int) and i == 0:
                    dve.wait_ge(qd_in, 16 * NT)
                row = flat(qd[:, at(i), :])
                dve.tensor_scalar(row, row, lane[:, 2:3], lane[:, 3:4], ALU.logical_shift_right, ALU.bitwise_and).then_inc(qd_unpacked, 1)

            def zeros():
                dve.wait_ge(zeros_in, 48)
                zb = zq[:, :].bitcast(U8)
                two = z8[:, 0:2 * NPAD].rearrange("p (a n) -> p a n", a=2)[:, :, 0:INTER].rearrange("p a (b h) -> p a b h", h=2)
                one = z8[:, 2 * NPAD:TABLE].rearrange("p (b h) -> p b h", h=2)
                for h in range(2):
                    dve.tensor_scalar(two[0:GI, :, :, h], zb[0:GI, 0:INTER].rearrange("p (a b) -> p a b", a=2),
                                      4 * h, 15, ALU.logical_shift_right, ALU.bitwise_and).then_inc(zeros_step, 1)
                    dve.tensor_scalar(one[0:GD, :, h], zb[0:GD, INTER:INTER + D // 2],
                                      4 * h, 15, ALU.logical_shift_right, ALU.bitwise_and).then_inc(zeros_step, 1)

            def index_step(part, n):
                groups = (GI, GD)[part]
                if n == 0:
                    if part == 0:
                        dve.wait_ge(idx_in, 32)
                    else:
                        dve.wait_ge(idx_down_in, 16)
                    dve.tensor_scalar(idx_f[part], idx_i[part], 0.0, float(groups), ALU.is_lt, ALU.mult).then_inc(idx_step, 1)
                elif n == 1:
                    dve.wait_ge(idx_step, 3 * part + 1)
                    dve.tensor_tensor(idx_f[part], idx_i[part], idx_f[part], ALU.add).then_inc(idx_step, 1)
                else:
                    dve.wait_ge(idx_step, 3 * part + 2)
                    dve.tensor_scalar(idx_f[part], idx_f[part], 0.0, float(groups - 1), ALU.max, ALU.min).then_inc(idx_step, 1)

            def onehots(part):
                dve.wait_ge(idx_step, 3 * part + 3)
                dve.wait_ge(lane_made, 4)
                if part == 0:
                    for tb in range(2):
                        dve.tensor_scalar(onehot[:, tb * D:(tb + 1) * D].rearrange("p (t h r) -> p t h r", t=KT, h=2),
                                          idx_f[0][:, tb * D:(tb + 1) * D].rearrange("p (r t h) -> p t h r", t=KT, h=2),
                                          pick[:, :], None, ALU.is_equal).then_inc(onehot_made, 1)
                else:
                    dve.memset(onehot[:, 2 * D + INTER:2 * D + NPAD], 0.0).then_inc(onehot_made, 1)
                    dve.tensor_scalar(onehot[:, 2 * D:2 * D + INTER], idx_f[1], pick[:, :], None, ALU.is_equal).then_inc(onehot_made, 1)

            def w_differences(i, tb):
                if isinstance(i, int):
                    dve.wait_ge(qw_unpacked, 2 * chunks_for(i))
                if isinstance(i, int) and i < 2:
                    dve.wait_ge(scalars_made, 3)
                    dve.wait_ge(onehot_made, 2)
                n = 2 * i + tb
                dve.wait_ge(gathered, n + 1)
                wait_if(dve, w_formed, n - 1)
                dve.tensor_tensor(diff[:, tb, :].rearrange("p (t n) -> p t n", t=KT),
                                  qw[:, tb, :].bitcast(U8).rearrange("p (n t) -> p t n", t=KT)[:, :, at(i * P, P)],
                                  z_ps.rearrange("p (t n) -> p t n", t=KT), ALU.subtract).then_inc(diff_made, 1)

            def w_products(i, u, tb):
                dve.wait_ge(diff_made, 2 * i + tb + 1)
                wait_if(dve, w_lo_made, i - 1)
                dve.scalar_tensor_tensor(out=w_f32[:, u, tb * D:(tb + 1) * D], in0=diff[:, tb, :], scalar=c_w[:, tb:tb + 1],
                                         in1=s_ps, op0=ALU.mult, op1=ALU.mult).then_inc(w_formed, 1)

            def dequant_gate_up(i, u, tb):
                w_differences(i, tb)
                w_products(i, u, tb)

            def dequant_down(i, u):
                dve.wait_ge(gathered, 2 * NT + i + 1)
                dve.wait_ge(w_formed, 2 * NT + i)
                dve.tensor_tensor(diff[:, 0, :], flat(qd[:, at(i), :]), z_ps, ALU.subtract).then_inc(diff_made, 1)
                dve.wait_ge(diff_made, 2 * NT + i + 1)
                dve.wait_ge(w_lo_made, NT + i - 1)
                dve.scalar_tensor_tensor(out=w_f32[:, u, 0:D], in0=diff[:, 0, :], scalar=c_w[:, 2:3], in1=s_ps,
                                         op0=ALU.mult, op1=ALU.mult).then_inc(w_formed, 1)

            def form_gated(n, u):
                dve.wait_ge(tanh_gate_made, n + 1)
                dve.scalar_tensor_tensor(out=gated[:, u, :], in0=gated[:, u, :], scalar=1.0, in1=gate_ps,
                                         op0=ALU.add, op1=ALU.mult).then_inc(gated_made, 1)

            def form_hidden(n, u):
                dve.wait_ge(up_ready, n + 1)
                dve.wait_ge(gated_made, n + 1)
                wait_if(dve, h_lo_made, n - 1)
                dve.scalar_tensor_tensor(out=h_f32[:, u, :], in0=gated[:, u, :], scalar=2.0 ** (KBITS - XBITS - WBITS - 1), in1=up_ps,
                                         op0=ALU.mult, op1=ALU.mult).then_inc(h_formed, 1)

            def attention_step(s):
                score_max(s)
                if s == 0:
                    own_tops()
                else:
                    ln_sums(*ln_of_step[s][0])
                invert_sum(s)
                if s >= 1:
                    ln_moments(*ln_of_step[s][0])
                normalise(s)
                if s == 0:
                    ln_sums(0, 2)
                    ln_moments(0, 2)
                    onehots(0)
                    residual(0)
                elif s == 1:
                    scalars(0)
                    ln_sums(1, 0)
                    scalars(1)
                    ln_sums(0, 4)
                    ln_moments(1, 0)
                    scalars(2)
                    ln_moments(0, 4)
                    scalars(3)
                    residual(1)
                else:
                    if s == 2:
                        unpack_gate_up(0)
                    w_differences((s - 2) // 2, s % 2)
                    if s + 3 < B:
                        ln_sums(0, s + 3)
                    w_products((s - 2) // 2, (s - 2) // 2, s % 2)
                    if s + 3 < B:
                        ln_moments(0, s + 3)
                    residual(s)
                    n_low(s - 2)
                    if s == 5:
                        unpack_gate_up(1)

            def mixed_tile(i, u, s):
                w_differences(i + 2, 0)
                if s < B:
                    score_max(s)
                w_products(i + 2, u, 0)
                if s <= B:
                    ln_sums(1, s - 1)
                if s < B:
                    invert_sum(s)
                if s <= B:
                    ln_moments(1, s - 1)
                if s < B:
                    normalise(s)
                if i < 3:
                    unpack_gate_up(i + 2)
                unpack_down(i)
                form_gated(i, u)
                if s < B:
                    residual(s)
                dequant_gate_up(i + 2, u, 1)
                n_low(s - 2)
                form_hidden(i, u)

            def first_half(i, u):
                if not isinstance(i, int) or i + 2 < NT:
                    dequant_gate_up(i + 2, u, 0)
                    dequant_gate_up(i + 2, u, 1)
                down_indices = isinstance(i, int) and i == NT - 2
                if down_indices:
                    index_step(1, 0)
                unpack_down(i)
                form_gated(i, u)
                if down_indices:
                    index_step(1, 1)
                form_hidden(i, u)
                if down_indices:
                    index_step(1, 2)
                    onehots(1)

            def second_half(i, u):
                dequant_down(i, u)
                form_gated(NT + i, u)
                form_hidden(NT + i, u)

            dve.memset(table_z[:, :].bitcast(I32), 0).then_inc(const_made, 1)
            for ln, b in ln_of_step[-1]:
                ln_sums(ln, b)
                ln_moments(ln, b)
            lanes()
            zeros()
            for n in range(3):
                index_step(0, n)
            for s in range(PURE):
                attention_step(s)
            run_first(dve, mixed_tile, first_half)
            dve.wait_ge(qd_unpacked, NT)
            run_second(dve, second_half)

            with dve.Fori(0, B) as m:
                dve.wait_ge(down_ready, m + 1)
                row = flat(x_sb[:, at(m), :])
                dve.scalar_tensor_tensor(out=row, in0=flat(psum[:, at(m), :]), scalar=tau, in1=row,
                                         op0=ALU.mult, op1=ALU.add).then_inc(out_formed, 1)

        @block.scalar
        def _(act):
            def copy_ctx(b):
                act.wait_ge(turned, 2 * b + 1)
                if b >= 2:
                    act.wait_ge(scored, b - 1)
                act.activation(ctxT[:, b % 2, :], ctxT_ps, ACT.Copy).then_inc(turned_copied, 1)

            def copy_query(b):
                act.wait_ge(turned, 2 * b + 2)
                if b >= 2:
                    act.wait_ge(scored, b - 1)
                act.activation(queryT[:, b % 2, :], queryT_ps, ACT.Copy, scale=SCALE).then_inc(turned_copied, 1)

            def make_query(b):
                act.wait_ge(shift_made, mv_count[0, b])
                if b >= 2:
                    act.wait_ge(turned, 2 * b - 2)
                act.activation(query[:, b % 2, :], x_sb[:, b, :], ACT.Identity, bias=shift[:, 0, b:b + 1],
                               scale=rstd[:, 0, b:b + 1]).then_inc(query_made, 1)

            def make_normed(b):
                act.wait_ge(shift_made, mv_count[1, b])
                if b >= 2:
                    act.wait_ge(n_turned, b - 1)
                act.activation(normed[:, b % 2, :].rearrange("p (t h r) -> p t h r", t=KT, h=2),
                               x_sb[:, b, :].rearrange("p (r t h) -> p t h r", t=KT, h=2), ACT.Identity,
                               bias=shift[:, 1, b:b + 1], scale=rstd[:, 1, b:b + 1]).then_inc(normed_made, 1)

            def part1(c):
                if c == 0:
                    act.wait_ge(rows_in, 16 * 6)
                if CHUNKS[c] is None:
                    act.wait_ge(rows_down_in, 16 * 3)
                act.activation(chunk(table_s, c), chunk(scale_rows, c), ACT.Copy).then_inc(part1_made, 1)

            def part2(c):
                act.wait_ge(rest1_made, c + 1)
                act.activation(chunk(table_s, c, 64), chunk(scale_rows, c, 64), ACT.Copy).then_inc(part2_made, 1)

            def zero_rows(c):
                act.wait_ge(zeros_step, 4)
                if CHUNKS[c] is None:
                    rows, here = table_z[0:GD, 2 * NPAD:TABLE], z8[0:GD, 2 * NPAD:TABLE]
                else:
                    lo, hi = CHUNKS[c]
                    rows, here = (tile[0:GI, 0:2 * NPAD].rearrange("p (a n) -> p a n", a=2)[:, :, lo:min(hi, INTER)]
                                  for tile in (table_z, z8))
                act.activation(rows, here, ACT.Copy, bias=1.0).then_inc(zeros_made, 1)

            def exponentials(b):
                act.wait_ge(max_made, b + 1)
                if b >= 2:
                    act.wait_ge(valued, b - 1)
                act.activation(probs[:, b % 2, :], score_bank(b), ACT.Exp, bias=smax[:, 0, b:b + 1],
                               accum_out=smax[:, 1, b:b + 1]).then_inc(exp_made, 1)

            def n_high(b):
                act.wait_ge(n_turned, b + 1)
                act.activation(nT_hi[:, :, b * S:(b + 1) * S], nT_ps.rearrange("p (t m) -> p t m", t=KT),
                               ACT.Copy, scale=2.0 ** XBITS).then_inc(n_hi_made, 1)

            def high_w_gate_up(i, u):
                act.wait_ge(w_formed, 2 * i + 2)
                act.activation(flat(w_hi[:, at(i), :, :]), w_f32[:, u, :], ACT.Copy).then_inc(w_hi_made, 1)

            def high_w_down(i, u):
                act.wait_ge(w_formed, 2 * NT + i + 1)
                act.activation(flat(wd[:, at(i), 0]), w_f32[:, u, 0:D], ACT.Copy).then_inc(w_hi_made, 1)

            def gate_tanh(n, u):
                act.wait_ge(gate_ready, n + 1)
                wait_if(act, h_formed, n - 1)
                act.activation(gated[:, u, :], gate_ps, ACT.Tanh, scale=tanh_scale).then_inc(tanh_gate_made, 1)

            def high_h(half, i, u):
                act.wait_ge(h_formed, half * NT + i + 1)
                act.activation(flat(hidden[:, half, at(i), 0, :]), h_f32[:, u, :], ACT.Copy).then_inc(h_hi_made, 1)

            def split_table(s):
                for c in range(len(CHUNKS)):
                    if s == SPLIT_STEP[c] + 1:
                        part2(c)
                        zero_rows(c)
                    if s == SPLIT_STEP[c]:
                        part1(c)

            def attention_step(s):
                exponentials(s)
                copy_query(s + 1)
                if s + 2 < B:
                    copy_ctx(s + 2)
                if s < 1:
                    split_table(s)
                if s >= 2:
                    n_high(s - 2)
                if s + 2 < B:
                    make_query(s + 2)
                if s == 1:
                    split_table(s)
                if s >= 1:
                    make_normed(s - 1)
                if s == 4:
                    high_w_gate_up(0, 0)
                if s >= 2:
                    split_table(s)

            def mixed_tile(i, u, s):
                if s < B:
                    exponentials(s)
                if i == 0:
                    high_w_gate_up(1, 1)
                gate_tanh(i, u)
                if s + 1 < B:
                    copy_query(s + 1)
                split_table(s)
                n_high(s - 2)
                high_w_gate_up(i + 2, u)
                high_h(0, i, u)
                if s <= B:
                    make_normed(s - 1)

            def first_half(i, u):
                if isinstance(i, int) and i == 4:
                    split_table(STEPS)
                gate_tanh(i, u)
                if not isinstance(i, int) or i + 2 < NT:
                    high_w_gate_up(i + 2, u)
                high_h(0, i, u)

            def second_half(i, u):
                high_w_down(i, u)
                gate_tanh(NT + i, u)
                high_h(1, i, u)

            copy_ctx(0)
            make_query(0)
            make_query(1)
            copy_query(0)
            copy_ctx(1)
            act.wait_ge(gates_in, 32)
            act.activation(tanhs[:, :], gates[:, :], ACT.Tanh).then_inc(tanh_made, 1)
            for s in range(PURE):
                attention_step(s)
            run_first(act, mixed_tile, first_half)
            run_second(act, second_half)

        @block.tensor
        def _(pe):
            def turn_ctx(b):
                pe.wait_ge(ctx_loaded[b], 16)
                if b >= 1:
                    pe.wait_ge(turned_copied, 2 * b - 1)
                for t in range(KT):
                    mm = pe.transpose(ctxT_ps[:, t * P:(t + 1) * P], ctx_sb[:, b, t * P:(t + 1) * P], ident[:, :])
                mm.then_inc(turned, 1)

            def turn_query(b):
                pe.wait_ge(query_made, b + 1)
                if b >= 1:
                    pe.wait_ge(turned_copied, 2 * b)
                for t in range(KT):
                    mm = pe.transpose(queryT_ps[:, t * P:(t + 1) * P], query[:, b % 2, t * P:(t + 1) * P], ident[:, :])
                mm.then_inc(turned, 1)

            def scores(b):
                pe.wait_ge(turned_copied, 2 * (b + 1))
                if b >= PURE:
                    pe.wait_ge(x2_made, b)
                for t in range(KT):
                    mm = pe.matmul(score_bank(b), queryT[:, b % 2, t * P:(t + 1) * P], ctxT[:, b % 2, t * P:(t + 1) * P],
                                   start=(t == 0), stop=(t == KT - 1))
                mm.then_inc(scored, 1)

            def values(b):
                pe.wait_ge(probs_made, b + 1)
                if 1 <= b < PURE:
                    pe.wait_ge(x2_made, b)
                pe.matmul(value_ps, probs[:, b % 2, :], ctx_sb[:, b, :], start=True, stop=True).then_inc(valued, 1)

            def turn_normed(b):
                pe.wait_ge(normed_made, b + 1)
                if b >= 1:
                    pe.wait_ge(n_lo_made, b)
                for t in range(KT):
                    mm = pe.transpose(nT_ps[:, t * P:(t + 1) * P], normed[:, b % 2, t * P:(t + 1) * P], ident[:, :])
                mm.then_inc(n_turned, 1)

            def gather_gate_up(i, tb):
                if isinstance(i, int) and tb == 0:
                    pe.wait_ge(part3_made, chunks_for(i))
                    pe.wait_ge(zeros_made, chunks_for(i))
                    if i == 0:
                        pe.wait_ge(onehot_made, 2)
                wait_if(pe, w_formed, 2 * i + tb)
                scale_cols = table_s[:, at(i * P + tb * NPAD, P)]
                zero_cols = table_z[:, at(i * P + tb * NPAD, P)]
                for t in range(KT):
                    k = slice(tb * D + t * P, tb * D + (t + 1) * P)
                    pe.matmul(s_ps[:, t * P:(t + 1) * P], onehot[:, k], scale_cols, start=True, stop=True)
                    mm = pe.matmul(z_ps[:, t * P:(t + 1) * P], onehot[0:32, k], zero_cols, start=True, stop=True)
                mm.then_inc(gathered, 1)

            def gather_down(i):
                pe.wait_ge(w_formed, 2 * NT + i)
                k = at(i * P + 2 * D, P)
                pe.matmul(s_ps, onehot[:, k], table_s[:, 2 * NPAD:TABLE], start=True, stop=True)
                pe.matmul(z_ps, onehot[0:32, k], table_z[:, 2 * NPAD:TABLE], start=True, stop=True).then_inc(gathered, 1)

            def project(half, i, tb):
                n = half * NT + i
                if tb == 0:
                    if half == 0:
                        pe.wait_ge(w_hi_made, i + 1)
                    wait_if(pe, gated_made, n)
                else:
                    wait_if(pe, h_formed, n)
                acc, tok = (gate_ps, up_ps)[tb], slice(half * HALF, (half + 1) * HALF)
                for t in range(KT):
                    hi = flat(w_hi[:, at(i), tb, t * P:(t + 1) * P])
                    pe.matmul(acc, hi, nT_hi[:, t, tok], start=(t == 0), stop=False)
                    pe.matmul(acc, hi, nT_lo[:, t, tok], start=False, stop=False)
                if half == 0 and tb == 0:
                    pe.wait_ge(w_lo_made, i + 1)
                for t in range(KT):
                    lo = flat(w_lo[:, at(i), tb, t * P:(t + 1) * P])
                    mm = pe.matmul(acc, lo, nT_hi[:, t, tok], start=False, stop=(t == KT - 1))
                mm.then_inc((gate_ready, up_ready)[tb], 1)

            def attention_step(s):
                scores(s)
                turn_query(s + 1)
                if s + 2 < B:
                    turn_ctx(s + 2)
                if s >= 2:
                    gather_gate_up((s - 2) // 2, s % 2)
                    turn_normed(s - 2)
                values(s)

            def mixed_tile(i, u, s):
                gather_gate_up(i + 2, 0)
                if s < B:
                    scores(s)
                if i == 0:
                    pe.wait_ge(n_lo_made, BH)
                project(0, i, 0)
                if s < B:
                    values(s)
                if s + 1 < B:
                    turn_query(s + 1)
                turn_normed(s - 2)
                gather_gate_up(i + 2, 1)
                project(0, i, 1)

            def first_half(i, u):
                for tb in range(2):
                    if not isinstance(i, int) or i + 2 < NT:
                        gather_gate_up(i + 2, tb)
                    project(0, i, tb)

            def second_half(i, u):
                gather_down(i)
                project(1, i, 0)
                project(1, i, 1)

            pe.wait_ge(ident_made, 2)
            turn_ctx(0)
            turn_query(0)
            turn_ctx(1)
            for s in range(PURE):
                attention_step(s)
            run_first(pe, mixed_tile, first_half)
            pe.wait_ge(part3_made, len(CHUNKS))
            pe.wait_ge(zeros_made, len(CHUNKS))
            pe.wait_ge(onehot_made, 4)
            pe.wait_ge(n_lo_made, B)
            run_second(pe, second_half)

            pe.wait_ge(w_lo_made, 2 * NT)
            for half in range(2):
                pe.wait_ge(h_lo_made, (half + 1) * NT)
                with pe.Fori(0, BH) as m:
                    acc = flat(psum[:, at(m + half * BH), :])
                    for i in range(NT):
                        hi = flat(hidden[:, half, i:i + 1, 0, at(m * P, P)])
                        lo = flat(hidden[:, half, i:i + 1, 1, at(m * P, P)])
                        pe.matmul(acc, hi, wd[:, i, 0], start=(i == 0), stop=False)
                        pe.matmul(acc, hi, wd[:, i, 1], start=False, stop=False)
                        mm = pe.matmul(acc, lo, wd[:, i, 0], start=False, stop=(i == NT - 1))
                    mm.then_inc(down_ready, 1)


_INS = ["x", "ctx_4096", "g_xattn", "g_ffn"] + [f"L0_ffn_{m}_{part}" for m in ("gate", "up", "down")
                                                 for part in ("qweight", "scales", "qzeros", "g_idx")]
_OUTS = [((8, 128, 512), "float32")]


def kernel(**inputs):
    import numpy as _np
    import concourse.bacc as _bacc
    from concourse import mybir as _mybir
    from concourse.bass_utils import run_bass_kernel_spmd as _run

    nc = _bacc.Bacc("TRN2", target_bir_lowering=False, num_devices=1)
    arrays, args = {}, []
    for name in _INS:
        a = _np.ascontiguousarray(inputs[name])
        arrays[f"in_{name}_dram"] = a
        args.append(nc.dram_tensor(f"in_{name}_dram", a.shape, _mybir.dt.from_np(a.dtype), kind="ExternalInput").ap())
    for n, (shape, dtype) in enumerate(_OUTS):
        dt = _mybir.dt.from_np(_np.dtype(dtype))
        args.append(nc.dram_tensor(f"out_{n}_dram", shape, dt, kind="ExternalOutput").ap())
    flamingo_gated_block(nc, *args)
    r = _run(nc, [arrays], core_ids=[0])
    return r.results[0]["out_0_dram"]
```
